# Optimizing a Trainium2 kernel written in Bass

```python
import numpy as np
import jax
import jax.numpy as jnp

def _softmax(x, axis=-1):
    return jax.nn.softmax(x, axis=axis)

def _gelu(x):
    return jax.nn.gelu(x, approximate=True)

def _silu(x):
    return jax.nn.silu(x)

def _sigmoid(x):
    return jax.nn.sigmoid(x)

def _layernorm(x, axis=-1, eps=1e-05):
    m = jnp.mean(x, axis=axis, keepdims=True)
    v = jnp.var(x, axis=axis, keepdims=True)
    return (x - m) / jnp.sqrt(v + eps)

def _scatter_add(tgt, idx, src, axis=0):
    return tgt.at[idx].add(src)

def _segment_sum(src, seg, n):
    return jax.ops.segment_sum(src, seg, n)
kernel_name = 'mk_macaron_d1_jaxref_r8_966a44'

def setup_inputs(seed: int=0):
    np.random.seed(seed)
    _w = jnp.asarray

    def _L0_attn_setup():
        import jax, jax.numpy as jnp
        import numpy as np
        HIDDEN = 256
        KEY_DIM = 256
        NUM_HEADS = 16
        EPS = 1e-05

        def rms_norm(x, w, eps=EPS):
            ms = jnp.mean(x * x, axis=-1, keepdims=True)
            return x * jax.lax.rsqrt(ms + eps) * w
        key = jax.random.key(seed)
        ks = jax.random.split(key, 6)
        bound = 1.0 / np.sqrt(HIDDEN)
        x = jax.random.normal(ks[0], (2, 256, HIDDEN), dtype=jnp.float32)
        rms_w = jnp.ones((HIDDEN,), dtype=jnp.float32)
        Wq = jax.random.uniform(ks[1], (HIDDEN, KEY_DIM), jnp.float32, -bound, bound)
        Wk = jax.random.uniform(ks[2], (HIDDEN, KEY_DIM), jnp.float32, -bound, bound)
        Wv = jax.random.uniform(ks[3], (HIDDEN, KEY_DIM), jnp.float32, -bound, bound)
        Wo = jax.random.uniform(ks[4], (KEY_DIM, HIDDEN), jnp.float32, -bound, bound)
        return {'x': x, 'rms_w': rms_w, 'Wq': Wq, 'Wk': Wk, 'Wv': Wv, 'Wo': Wo}
    _L0_attn_in = _L0_attn_setup()

    def _L0_ffn_setup():
        import jax, jax.numpy as jnp
        import numpy as np
        B, S, D, FF, E = (4, 256, 256, 1024, 2)
        key = jax.random.key(seed)
        k0, k1, k2, k3, k4 = jax.random.split(key, 5)
        s = 0.02
        return {'hidden_states': jax.random.normal(k0, (B, S, D), jnp.float32), 'gate_w': jax.random.normal(k1, (E, D), jnp.float32) * s, 'w_gate': jax.random.normal(k2, (E, FF, D), jnp.float32) * s, 'w_up': jax.random.normal(k3, (E, FF, D), jnp.float32) * s, 'w_down': jax.random.normal(k4, (E, D, FF), jnp.float32) * s}
    _L0_ffn_in = _L0_ffn_setup()
    _d = {'L0_attn_x': _L0_attn_in['x'], 'L0_attn_rms_w': _L0_attn_in['rms_w'], 'L0_attn_Wq': _L0_attn_in['Wq'], 'L0_attn_Wk': _L0_attn_in['Wk'], 'L0_attn_Wv': _L0_attn_in['Wv'], 'L0_attn_Wo': _L0_attn_in['Wo'], 'L0_ffn_gate_w': _L0_ffn_in['gate_w'], 'L0_ffn_w_gate': _L0_ffn_in['w_gate'], 'L0_ffn_w_up': _L0_ffn_in['w_up'], 'L0_ffn_w_down': _L0_ffn_in['w_down']}
    _x0 = _d['L0_attn_x']
    _d['L0_attn_x'] = jax.random.normal(jax.random.fold_in(jax.random.key(seed), 1), (8, 512, 256), dtype=_x0.dtype)
    del _x0
    return _d

def reference(L0_attn_x, L0_attn_rms_w, L0_attn_Wq, L0_attn_Wk, L0_attn_Wv, L0_attn_Wo, L0_ffn_gate_w, L0_ffn_w_gate, L0_ffn_w_up, L0_ffn_w_down):

    def _L0_attn_ref(x, rms_w, Wq, Wk, Wv, Wo):
        import jax, jax.numpy as jnp
        import numpy as np
        HIDDEN = 256
        KEY_DIM = 256
        NUM_HEADS = 16
        EPS = 1e-05

        def rms_norm(x, w, eps=EPS):
            ms = jnp.mean(x * x, axis=-1, keepdims=True)
            return x * jax.lax.rsqrt(ms + eps) * w
        B, S, _ = x.shape
        residual = x
        xn = rms_norm(x, rms_w)
        q = (xn @ Wq).reshape(B, S, NUM_HEADS, KEY_DIM // NUM_HEADS)
        k = (xn @ Wk).reshape(B, S, NUM_HEADS, KEY_DIM // NUM_HEADS)
        v = (xn @ Wv).reshape(B, S, NUM_HEADS, KEY_DIM // NUM_HEADS)
        scale = 1.0 / jnp.sqrt(jnp.float32(KEY_DIM))
        scores = jnp.einsum('bshd,bthd->bhst', q, k) * scale
        causal = jnp.tril(jnp.ones((S, S), dtype=bool))
        scores = jnp.where(causal[None, None], scores, -jnp.inf)
        probs = jax.nn.softmax(scores, axis=-1)
        out = jnp.einsum('bhst,bthd->bshd', probs, v).reshape(B, S, KEY_DIM)
        return out @ Wo + residual

    def _L0_ffn_ref(hidden_states, gate_w, w_gate, w_up, w_down):
        import jax, jax.numpy as jnp
        import numpy as np
        B, S, D, FF, E = (4, 256, 256, 1024, 2)
        b, s, d = hidden_states.shape
        x = hidden_states.reshape(-1, d)
        logits = x @ gate_w.T
        probs = jax.nn.softmax(logits.astype(jnp.float32), axis=-1)
        sel = jnp.argmax(probs, axis=-1)
        top_w = jnp.take_along_axis(probs, sel[:, None], axis=-1)
        onehot = jax.nn.one_hot(sel, gate_w.shape[0], dtype=x.dtype)
        g = jnp.einsum('td,efd->etf', x, w_gate)
        u = jnp.einsum('td,efd->etf', x, w_up)
        h = jax.nn.silu(g) * u
        y = jnp.einsum('etf,edf->etd', h, w_down)
        out = jnp.einsum('etd,te->td', y, onehot * top_w)
        return out.reshape(b, s, d)
    x = L0_attn_x
    x = x + 0.5 * _L0_ffn_ref(_layernorm(x, axis=-1), L0_ffn_gate_w, L0_ffn_w_gate, L0_ffn_w_up, L0_ffn_w_down)
    x = x + _L0_attn_ref(_layernorm(x, axis=-1), L0_attn_rms_w, L0_attn_Wq, L0_attn_Wk, L0_attn_Wv, L0_attn_Wo)
    x = x + 0.5 * _L0_ffn_ref(_layernorm(x, axis=-1), L0_ffn_gate_w, L0_ffn_w_gate, L0_ffn_w_up, L0_ffn_w_down)
    return x

_drawn_inputs = setup_inputs


def setup_inputs(seed=0):
    import zlib

    import numpy as np

    out = dict(_drawn_inputs(seed))
    spreads = {'L0_attn_rms_w': (1.0, 0.6)}
    factors = {'L0_attn_Wq': 8.0,
     'L0_attn_Wk': 8.0,
     'L0_attn_Wv': 2.836,
     'L0_attn_Wo': 2.777,
     'L0_ffn_gate_w': 5.196,
     'L0_ffn_w_gate': 3.817,
     'L0_ffn_w_up': 3.774,
     'L0_ffn_w_down': 3.773}
    for name, (base, spread) in spreads.items():
        noise = np.random.default_rng([zlib.crc32(name.encode()), seed]).standard_normal(out[name].shape)
        drawn = base * np.exp(spread * noise) if base else spread * noise
        out[name] = jnp.asarray(drawn.astype(out[name].dtype))
    for name, factor in factors.items():
        out[name] = (out[name] * factor).astype(out[name].dtype)
    return out
```

```python
from contextlib import ExitStack

import concourse.bass as bass
from concourse import mybir

F32 = mybir.dt.float32
F32R = mybir.dt.float32r
BF16 = mybir.dt.bfloat16
F16 = mybir.dt.float16
ALU = mybir.AluOpType
ACT = mybir.ActivationFunctionType

P = 128
B, S, D = 8, 512, 256
E, FF = 2, 1024
H = 16
HD = D // H
T = S // P
KB = D // P
FB = FF // P
UNITS = E * FB
EPS = 1e-5
QSCALE = -1.0 / 16.0
HUGE = 3e38
TWO_ONES = 1.0 + 0x3F80 / 2**23
QPART = [0, 1, 2, 0, 1, 0]
KPART = [0, 0, 0, 1, 1, 2]
ROWS = HD * len(QPART)
VW = 3 * HD + 1
FILLS = 3 * H
GROUPS = 2
HG = H // GROUPS
PER_SLOT = 5
WQ, WK, WV, WO = 0, D, 2 * D, 3 * D
PIECES = 3 * E + 1
STAGES = 4

S_FILLS = [[(3, 0)], [(2, 0), (0, 384)], [(1, 0)]]
ST_FILLS = [[(0, 0)], [(1, 0), (3, 384)], [(2, 0)]]
ST_WIDTH = [512, 512, 256]

DVE_LINKS = {"start": 8, "A0": 0, "A": 12, "B0": 14, "B": 14, "B7": 6}
POOL_LINKS = {"start": 5, "A0": 0, "A": 1, "B0": 6, "B": 6, "B7": 5}


def half_a(k, ffn, attend):
    extra = [[] for _ in range(UNITS)]
    fills = []
    if attend:
        for f in range(FILLS + 2):
            now = []
            if f < FILLS:
                now += [("scores_t", f), ("exp", f), ("causal", f)]
            if 1 <= f <= FILLS:
                now += [("p_split", f - 1)]
            if f >= 2:
                now += [("pv", f - 2)]
                if (f - 2) % (3 * HG) == 3 * HG - 1:
                    now += [("o_norm", (f - 2) // (3 * HG))]
            fills.append(now)
        extra[12] += [("transpose", "o")]
        extra[13] += [("out_proj", 0), ("out_proj", 1), ("stats", "second"), ("norm", "second")]
        extra[14] += [("transpose", "second"), ("route_a", "second")]
        extra[15] += [("route_b", "second")]
    if ffn and isinstance(k, int) and k == 0:
        for n, s in ((2, 0), (3, 2), (4, 3), (5, 5), (6, 6)):
            extra[s] += [("weights", n)]
    return steps("A", k, ffn, extra, fills, 1)


def half_b(k, ffn, project, ahead):
    extra = [[] for _ in range(UNITS)]
    fills = []
    if project:
        extra[0] += [("stats", "attn"), ("norm", "attn")]
        extra[1] += [("transpose", "attn")]
        extra[2] += [("proj", 0), ("proj", 1), ("proj_rest", 0), ("proj_rest", 1), ("qk_in", 0)]
        extra[3] += [("proj", 2), ("proj", 3), ("proj_rest", 2), ("proj_rest", 3), ("qk_in", 1)]
        extra[4] += [("proj", 4), ("proj", 5), ("proj_rest", 4), ("proj_rest", 5)]
        fills = [[("scores", f)] for f in range(FILLS)]
        if ahead:
            extra[8] += [("stats", "first"), ("norm", "first")]
            extra[9] += [("transpose", "first"), ("route_a", "first")]
            extra[10] += [("route_b", "first")]
        extra[15] += [("row_max", 0)]
    return steps("B", k, ffn, extra, fills, 5)


def steps(half, k, ffn, extra, fills, first):
    out = []
    fills = list(fills)
    pending = not (isinstance(k, int) and (half, k) in (("A", 0), ("A", 1), ("B", B)))
    for s in range(UNITS):
        def fill():
            if s >= first and fills:
                out.extend(fills.pop(0))
        down = s > 0 and ffn or s == 0 and pending
        if ffn:
            out.append(("gate", s))
        fill()
        if ffn:
            out.append(("up", s))
        fill()
        for i in range(T):
            if down:
                out.append(("down", s - 1, i))
            if i % 2:
                fill()
        if down and s in (0, FB):
            out.append(("x_update", s - 1))
        fill()
        out.extend(extra[s])
        if ffn:
            out.append(("h_split", s))
    while fills:
        out.extend(fills.pop(0))
    return out


class Round:

    def __init__(self, k):
        self.k = k
        self.fixed = isinstance(k, int)
        self.first = self.fixed and k == 0
        self.last = self.fixed and k == B

    def unit(self, half):
        if half == "A":
            return 0 if self.first else 32 * self.k - 16
        return 240 if self.last else 16 if self.first else 32 * self.k

    def batch(self, half):
        return self.k - 1 if half == "A" else self.k

    def transposed(self, what):
        if what == "first":
            return 2 if self.first else 4 * self.k + 2
        if what == "attn":
            return 1 if self.first else 4 * self.k + 1
        short = 1 if self.last else 0
        return 4 * self.k - 1 - short if what == "o" else 4 * self.k - short

    def normed(self, what):
        if what == "first":
            return 2 if self.first else 3 * self.k + 2
        if what == "attn":
            return 1 if self.first else 3 * self.k + 1
        return 3 * self.k - (1 if self.last else 0)

    def routed(self, what):
        if what == "first":
            return 1 if self.first else 2 * self.k + 1
        return 2 * self.k - (1 if self.last else 0)


class Start(Round):

    def __init__(self):
        Round.__init__(self, 0)

    def transposed(self, what):
        return 0

    def normed(self, what):
        return 0

    def routed(self, what):
        return 0


class Links:

    def __init__(self, eng, sem, per_part):
        self.eng, self.sem, self.per = eng, sem, per_part
        self.base, self.n, self.part = 0, 0, "start"

    def __call__(self, ins):
        self.n += 1
        ins.then_inc(self.sem, 1)
        self.eng.wait_ge(self.sem, self.base + self.n)

    def enter(self, part, k):
        assert self.n == self.per[self.part], (self.part, self.n)
        p = self.per
        before = p["start"]
        if part != "A0":
            before = before + p["A0"]
            if part != "B0":
                before = before + p["B0"] + (k - 1) * (p["A"] + p["B"])
                if part in ("B", "B7"):
                    before = before + p["A"]
        if part == "A" and isinstance(k, int) and k == B:
            before = before - p["B"] + p["B7"]
        self.base, self.n, self.part = before, 0, part


def macaron(nc, x, rms_w, gate_w, w_gate, w_up, w_down, w_attn, out):
    with ExitStack() as ctx:
        def sb(name, shape, dt):
            return ctx.enter_context(nc.sbuf_tensor(name, shape, dt))

        def sem(name):
            return ctx.enter_context(nc.semaphore(name))

        wg_hi = sb("wg_hi", [P, E, KB, FF], F32R)
        wg_lo = sb("wg_lo", [P, E, KB, FF], F32R)
        wu_hi = sb("wu_hi", [P, E, KB, FF], F32R)
        wu_lo = sb("wu_lo", [P, E, KB, FF], F32R)
        wd_hi = sb("wd_hi", [P, E, FB, D], F32R)
        wd_lo = sb("wd_lo", [P, E, FB, D], F32R)
        wa_hi = sb("wa_hi", [P, KB, 4 * D], F32R)
        wa_lo = sb("wa_lo", [P, KB, 4 * D], F32R)
        x_a = sb("x_a", [P, T, D], F32)
        x_b = sb("x_b", [P, T, D], F32)
        x_c = sb("x_c", [P, T, D], F32)
        xt_a_hi = sb("xt_a_hi", [P, KB, S], F32R)
        xt_a_lo = sb("xt_a_lo", [P, KB, S], F32R)
        xt_b_hi = sb("xt_b_hi", [P, KB, S], F32R)
        xt_b_lo = sb("xt_b_lo", [P, KB, S], F32R)
        hid = sb("hid", [P, 2, S], F32)
        h_hi = sb("h_hi", [P, S], F32R)
        h_lo = sb("h_lo", [P, S], F32R)
        qt = sb("qt", [P, H, S], BF16)
        kt = sb("kt", [P, H, S], BF16)
        v_parts = sb("v_parts", [P, T, H, VW], BF16)
        p_words, split_words, o_words = 2 * S, 3 * S, T * HG * VW
        area = sb("area", [P, p_words + split_words + o_words], F32)
        p_f32 = area[:, 0:p_words].rearrange("p (r n) -> p r n", r=2)
        p_f16 = area[:, p_words:p_words + split_words].bitcast(F16)
        p_hi = p_f16[:, 0:3 * S].rearrange("p (r n) -> p r n", r=3)
        p_lo = p_f16[:, 3 * S:6 * S].rearrange("p (r n) -> p r n", r=3)
        o_raw = area[:, p_words + split_words:].rearrange("p (i h c) -> p i h c", i=T, h=HG)
        xn = area[:, 0:T * D].rearrange("p (i d) -> p i d", i=T)
        rest = area[:, 0:2 * S].rearrange("p (r n) -> p r n", r=2)
        qk_parts = area[:, 2 * S:2 * S + 6 * S].bitcast(BF16).rearrange("p (c r n) -> p c r n", c=4, r=3)
        ident = sb("ident", [P, P], F32)
        mask = sb("mask", [P, S], BF16)
        w_diff = sb("w_diff", [P, 2, D], F32)
        rms_col = sb("rms_col", [P, KB], F32)
        minus_half = sb("minus_half", [P, T], F32)
        bn6 = sb("bn6", [P, T, 6], F32)
        mean_var = sb("mean_var", [P, T, 2], F32)
        rstd = sb("rstd", [P, T], F32)
        rms_scale = sb("rms_scale", [P, T], F32)
        tmp_pool = sb("tmp_pool", [P, T], F32)
        dlogit = sb("dlogit", [P, T], F32)
        neg_abs = sb("neg_abs", [P, T], F32)
        e_abs = sb("e_abs", [P, T], F32)
        prob = sb("prob", [P, T], F32)
        coef_a = sb("coef_a", [P, E, T], F32)
        coef_b = sb("coef_b", [P, E, T], F32)
        row_min = sb("row_min", [P, P], F32)
        max_parts = sb("max_parts", [P, 3, P], BF16)
        junk = w_diff[:, 1, :]
        recip = sb("recip", [P, T, HG], F32)

        ps_g = ctx.enter_context(nc.psum_tensor("ps_g", [P, S], F32))
        ps_u = ctx.enter_context(nc.psum_tensor("ps_u", [P, S], F32))
        ps_y = ctx.enter_context(nc.psum_tensor("ps_y", [P, T, D], F32))
        ps_t = ctx.enter_context(nc.psum_tensor("ps_t", [P, KB, S], F32))
        ps_r = ctx.enter_context(nc.psum_tensor("ps_r", [P, 2, S], F32))
        ps_o = ps_t[:, 1, 0:T * VW]
        ps_m = ps_t[:, 0, 0:P]

        qk_scratch = nc.dram_tensor("qk_scratch", [4, 3, HG, HD, S], BF16, kind="Internal").ap()
        max_scratch = nc.dram_tensor("max_scratch", [3, T, H, P], BF16, kind="Internal").ap()

        w_in = [sem(f"w_in{n}") for n in range(PIECES)]
        small_in, x_in, x_out = sem("small_in"), sem("x_in"), sem("x_out")
        qk_saved, max_saved, max_in = sem("qk_saved"), sem("max_saved"), sem("max_in")
        qk_loaded = [sem(f"qk_loaded{g}") for g in range(GROUPS)]
        const_ready, ones_ready, diff_ready = sem("const_ready"), sem("ones_ready"), sem("diff_ready")
        w_hi_done, w_ready = sem("w_hi_done"), sem("w_ready")
        stats_done, rstd_done, xn_ready = sem("stats_done"), sem("rstd_done"), sem("xn_ready")
        t_done, xt_hi_done, xt_lo_done = sem("t_done"), sem("xt_hi_done"), sem("xt_lo_done")
        dlogit_done, e_abs_done = sem("dlogit_done"), sem("e_abs_done")
        g_done, u_done, tanh_done = sem("g_done"), sem("u_done"), sem("tanh_done")
        gated, h_done = sem("gated"), sem("h_done")
        h_hi_done, h_lo_done = sem("h_hi_done"), sem("h_lo_done")
        down_done, x_updated = sem("down_done"), sem("x_updated")
        proj_done, part1_done, rest_done, part2_done, part3_done = (
            sem("proj_done"), sem("part1_done"), sem("rest_done"), sem("part2_done"), sem("part3_done"))
        s_done, max_done, mt_done, max_parts_done = (
            sem("s_done"), sem("max_done"), sem("mt_done"), sem("max_parts_done"))
        st_done, exp_done, causal_done = sem("st_done"), sem("exp_done"), sem("causal_done")
        p_hi_done, p_lo_done, pv_done = sem("p_hi_done"), sem("p_lo_done"), sem("pv_done")
        o_copied, o_normed, wo_done, x_c_ready = sem("o_copied"), sem("o_normed"), sem("wo_done"), sem("x_c_ready")
        dve_link, pool_link = sem("dve_link"), sem("pool_link")
        met_waits = {nc.vector: sem("dve_met"), nc.gpsimd: sem("pool_met"), nc.sync: sem("sp_met")}

        stage = [
            (qt if n < 2 else kt)[:, 8 * (n % 2):8 * (n % 2) + 8, :].bitcast(F32).rearrange("p h n -> p (h n)")
            for n in range(STAGES)
        ]
        raw = [w for e in range(E) for w in (w_gate[:, e], w_up[:, e], w_down[:, e])] + [w_attn]
        split = [(hi[:, e], lo[:, e]) for e in range(E)
                 for hi, lo in ((wg_hi, wg_lo), (wu_hi, wu_lo), (wd_hi, wd_lo))] + [(wa_hi[:], wa_lo[:])]

        def flat(ap):
            return ap.rearrange("p a b -> p (a b)")

        def xt_of(what):
            return (xt_a_hi, xt_a_lo) if what in ("first", "attn") else (xt_b_hi, xt_b_lo)

        def source(what):
            return {"first": x_a, "attn": x_b, "second": x_c}[what]

        def diag(ap):
            return ap.rearrange("p (a b) -> p a b", b=P)[:, 0:4:3, :]

        block = ctx.enter_context(nc.Block())

        def run(eng, emit, enter=None):
            def part(name, half, r, stages):
                if enter:
                    enter(name, r.k)
                for st in stages:
                    emit(half, r, st)

            first = Round(0)
            part("A0", "A", first, half_a(0, True, False))
            part("B0", "B", first, half_b(0, False, True, True))
            r = Round(1)
            part("A", "A", r, half_a(1, True, True))
            part("B", "B", r, half_b(1, True, True, True))
            with eng.Fori(2, B - 1) as k:
                r = Round(k)
                part("A", "A", r, half_a(k, True, True))
                part("B", "B", r, half_b(k, True, True, True))
            r = Round(B - 1)
            part("A", "A", r, half_a(B - 1, True, True))
            part("B7", "B", r, half_b(B - 1, True, True, False))
            r = Round(B)
            part("A", "A", r, half_a(B, False, True))
            for st in half_b(B, True, False, False):
                emit("B", r, st)
            for i in range(T):
                emit("end", r, ("down", UNITS - 1, i))
            emit("end", r, ("x_update", UNITS - 1))

        start_stages = [("weights", 0), ("stats", "first"), ("norm", "first"), ("transpose", "first"),
                        ("weights", 1), ("route_a", "first"), ("route_b", "first")]

        def pass_of(r, half):
            if half == "A":
                return 0 if r.first else 2 * r.k - 1
            return 15 if r.last else 2 * r.k

        def met(eng):
            eng.sem_inc(met_waits[eng], 1)

        def down_unit(half, r, s):
            base = r.unit("B") if half == "end" else r.unit(half)
            return base + s, s % UNITS

        @block.sync
        def _(sp):
            def batch_view(ap, n):
                return ap[bass.ds(n, 1)].rearrange("o (i p) d -> p (o i) d", p=P)

            sp.dma_start(x_a[:], batch_view(x, 0)).then_inc(x_in, 16)
            sp.dma_start(w_diff[:], gate_w.partition_broadcast(P)).then_inc(small_in, 16)
            sp.dma_start(rms_col[:], rms_w).then_inc(small_in, 16)
            for n in range(PIECES):
                if n >= STAGES:
                    sp.wait_ge(w_ready, n - STAGES + 1)
                sp.dma_start(stage[n % STAGES], flat(raw[n])).then_inc(w_in[n], 16)

            def emit(half, r, st):
                a = r.batch(half) if half != "end" else None
                if st[0] == "x_update":
                    u, s = down_unit(half, r, st[1])
                    if s != UNITS - 1:
                        return
                    if half == "B":
                        if not (r.last or r.fixed and r.k == B - 1):
                            sp.wait_ge(x_updated, 2 * pass_of(r, "A") + 2)
                            met(sp)
                            sp.dma_start(x_a[:], batch_view(x, r.k + 1)).then_inc(x_in, 16)
                    else:
                        done = 15 if half == "end" else None
                        n = B - 1 if half == "end" else r.k - 2
                        if half == "end":
                            sp.wait_ge(x_updated, 2 * (done + 1))
                        else:
                            sp.wait_ge(x_updated, 2 * (2 * r.k - 2) + 2)
                            met(sp)
                        sp.dma_start(batch_view(out, n), x_c[:]).then_inc(x_out, 16)
                elif st[0] == "proj_rest" and st[1] < 4:
                    c = st[1]
                    sp.wait_ge(part3_done, 6 * a + c + 1)
                    sp.dma_start(qk_scratch[c].rearrange("r h d t -> (h d) r t"),
                                 qk_parts[:, c]).then_inc(qk_saved, 16)
                elif st[0] == "qk_in":
                    g = st[1]
                    sp.wait_ge(qk_saved, 16 * (4 * a + 2 * g + 2))
                    met(sp)
                    if g == 0:
                        if r.first:
                            sp.wait_ge(w_ready, PIECES)
                        else:
                            sp.wait_ge(st_done, FILLS * a)
                    for n in range(len(QPART)):
                        rows = slice(HD * n, HD * n + HD)
                        heads = slice(HG * g, HG * g + HG)
                        sp.dma_start(qt[rows, heads, :], qk_scratch[2 * g, QPART[n]].rearrange(
                            "h d t -> d h t")).then_inc(qk_loaded[g], 16)
                        sp.dma_start(kt[rows, heads, :], qk_scratch[2 * g + 1, KPART[n]].rearrange(
                            "h d t -> d h t")).then_inc(qk_loaded[g], 16)
                elif st[0] == "row_max":
                    sp.wait_ge(max_parts_done, a + 1)
                    sp.dma_start(max_scratch.rearrange("r i h s -> (i h) r s"),
                                 max_parts[0:T * H]).then_inc(max_saved, 16)
                    sp.wait_ge(max_saved, 16 * (a + 1))
                    for n in range(3):
                        sp.dma_start(qt[ROWS + n:ROWS + n + 1].rearrange("o h (i s) -> o h i s", i=T),
                                     max_scratch[n:n + 1].rearrange("o i h s -> o h i s")
                                     ).then_inc(max_in, 16)

            run(sp, emit)
            sp.wait_ge(x_out, 16 * B)

        @block.gpsimd
        def _(pool):
            link = Links(pool, pool_link, POOL_LINKS)
            link(pool.memset(ident[:], 0.0))
            link(pool.affine_select(out=ident[:], in_=ident[:], compare_op=ALU.not_equal, fill=1.0,
                                    base=0, pattern=[[-1, P]], channel_multiplier=1))
            link(pool.memset(mask[:], 0.0))
            link(pool.affine_select(out=mask[:, S - P:S], in_=mask[:, S - P:S], compare_op=ALU.is_ge,
                                    fill=HUGE, base=0, pattern=[[-1, P]], channel_multiplier=1))
            pool.memset(minus_half[:], -0.5)
            pool.memset(v_parts[:], 1.0)
            pool.memset(row_min[:], 0.0).then_inc(const_ready, 1)
            pool.wait_ge(const_ready, 1)

            def emit(half, r, st):
                if st[0] == "stats":
                    n = r.normed(st[1])
                    pool.wait_ge(stats_done, n + 1)
                    met(pool)
                    var = mean_var[:, :, 1]
                    link(pool.tensor_scalar(tmp_pool[:], var, EPS, None, ALU.add))
                    ins = pool.tensor_tensor(rstd[:], tmp_pool[:], minus_half[:], ALU.pow)
                    if st[1] == "attn":
                        link(ins)
                        link(pool.tensor_tensor(tmp_pool[:], rstd[:], rstd[:], ALU.mult))
                        link(pool.tensor_tensor(tmp_pool[:], tmp_pool[:], var, ALU.mult))
                        met(pool)
                        link(pool.tensor_scalar(tmp_pool[:], tmp_pool[:], EPS, None, ALU.add))
                        ins = pool.tensor_tensor(rms_scale[:], tmp_pool[:], minus_half[:], ALU.pow)
                    ins.then_inc(rstd_done, 1)
                elif st[0] == "weights" and st[1] == PIECES - 1:
                    pool.wait_ge(w_ready, PIECES)
                    pool.wait_ge(h_lo_done, 6)
                    pool.memset(kt[ROWS:ROWS + 3].bitcast(F32), TWO_ONES).then_inc(ones_ready, 1)
                    pool.wait_ge(ones_ready, 1)
                elif st[0] == "h_split":
                    u = r.unit(half) + st[1]
                    pool.wait_ge(h_hi_done, u + 1)
                    pool.tensor_tensor(h_lo[:], hid[:, st[1] % 2, :], h_hi[:].bitcast(F32),
                                       ALU.subtract).then_inc(h_lo_done, 1)
                elif st[0] == "causal":
                    f = st[1]
                    pool.wait_ge(exp_done, FILLS * r.batch(half) + f + 1)
                    met(pool)
                    p = p_f32[:, f % 2, :]
                    p = diag(p) if f % 3 == 1 else p[:, 0:P]
                    pool.affine_select(out=p, in_=p, compare_op=ALU.is_ge, fill=0.0, base=0,
                                       pattern=[[0, 2], [1, P]] if f % 3 == 1 else [[1, P]],
                                       channel_multiplier=-1).then_inc(causal_done, 1)

            for st in start_stages:
                emit("start", Start(), st)
            run(pool, emit, link.enter)

        @block.scalar
        def _(act):
            def emit(half, r, st):
                what = st[0]
                if what == "weights":
                    n = st[1]
                    act.wait_ge(w_in[n], 16)
                    act.activation(flat(split[n][0]), stage[n % STAGES], ACT.Copy).then_inc(w_hi_done, 1)
                elif what == "transpose":
                    n = r.transposed(st[1])
                    if half == "start" or r.first and st[1] == "attn":
                        act.wait_ge(small_in, 32)
                    for kb in range(KB):
                        act.wait_ge(t_done, 2 * n + kb + 1)
                        scale = rms_col[:, kb:kb + 1] if st[1] == "attn" else 1.0
                        act.activation(xt_of(st[1])[0][:, kb, :], ps_t[:, kb, :], ACT.Copy,
                                       scale=scale).then_inc(xt_hi_done, 1)
                elif what == "route_a":
                    act.wait_ge(dlogit_done, r.routed(st[1]) + 1)
                    act.activation(e_abs[:], neg_abs[:], ACT.Exp).then_inc(e_abs_done, 1)
                elif what == "gate":
                    u = r.unit(half) + st[1]
                    act.wait_ge(g_done, u + 1)
                    if not (r.first and half == "A" and st[1] < 2):
                        act.wait_ge(h_lo_done, u - 1)
                    act.activation(hid[:, st[1] % 2, :], ps_g[:], ACT.Tanh, scale=0.5).then_inc(tanh_done, 1)
                elif what == "h_split":
                    u = r.unit(half) + st[1]
                    act.wait_ge(h_done, u + 1)
                    act.wait_ge(down_done, u)
                    act.activation(h_hi[:], hid[:, st[1] % 2, :], ACT.Copy).then_inc(h_hi_done, 1)
                elif what == "proj":
                    a, c = r.batch(half), st[1]
                    act.wait_ge(proj_done, 6 * a + c + 1)
                    if c < 4:
                        act.activation(qk_parts[:, c, 0, :], ps_r[:, c % 2, :], ACT.Copy,
                                       scale=1.0 if c % 2 else QSCALE).then_inc(part1_done, 1)
                    else:
                        act.activation(v_parts[:, 2 * (c - 4):2 * (c - 4) + 2, :, 0:HD],
                                       ps_r[:, c % 2, :].rearrange("p (i h d) -> p i h d", i=2, h=H),
                                       ACT.Copy).then_inc(part1_done, 1)
                elif what == "proj_rest":
                    a, c = r.batch(half), st[1]
                    act.wait_ge(rest_done, 6 * a + c + 1)
                    if c < 4:
                        act.activation(qk_parts[:, c, 1, :], rest[:, c % 2, :], ACT.Copy).then_inc(part2_done, 1)
                    else:
                        act.activation(v_parts[:, 2 * (c - 4):2 * (c - 4) + 2, :, HD:2 * HD],
                                       rest[:, c % 2, :].rearrange("p (i h d) -> p i h d", i=2, h=H),
                                       ACT.Copy).then_inc(part2_done, 1)
                elif what == "exp":
                    a, f = r.batch(half), st[1]
                    act.wait_ge(st_done, FILLS * a + f + 1)
                    if f >= 2 or not (r.fixed and r.k == 1):
                        act.wait_ge(p_lo_done, FILLS * a + f - 1)
                    n = ST_WIDTH[f % 3]
                    act.activation(p_f32[:, f % 2, 0:n], ps_r[:, f % 2, 0:n], ACT.Exp,
                                   scale=-1.0).then_inc(exp_done, 1)
                elif what == "p_split":
                    a, f = r.batch(half), st[1]
                    act.wait_ge(causal_done, FILLS * a + f + 1)
                    if f >= 3 or not (r.fixed and r.k == 1):
                        act.wait_ge(pv_done, FILLS * a + f - 2)
                    n = ST_WIDTH[f % 3]
                    act.activation(p_hi[:, f % 3, 0:n], p_f32[:, f % 2, 0:n], ACT.Copy).then_inc(p_hi_done, 1)
                elif what == "pv" and st[1] % 3 == 2:
                    a, h = r.batch(half), st[1] // 3
                    act.wait_ge(pv_done, FILLS * a + 3 * h + 3)
                    if h % HG == 0:
                        act.wait_ge(o_normed, 2 * a + h // HG)
                    act.activation(o_raw[:, :, h % HG, :], ps_o.rearrange("p (i c) -> p i c", i=T),
                                   ACT.Copy).then_inc(o_copied, 1)

            for st in start_stages:
                emit("start", Start(), st)
            run(act, emit)

        @block.vector
        def _(dve):
            link = Links(dve, dve_link, DVE_LINKS)
            dve.wait_ge(small_in, 32)
            dve.tensor_tensor(w_diff[:, 0, :], w_diff[:, 0, :], w_diff[:, 1, :],
                              ALU.subtract).then_inc(diff_ready, 1)
            dve.wait_ge(diff_ready, 1)

            def emit(half, r, st):
                what = st[0]
                if what == "weights":
                    n = st[1]
                    dve.wait_ge(w_hi_done, n + 1)
                    dve.tensor_tensor(flat(split[n][1]), stage[n % STAGES], flat(split[n][0]).bitcast(F32),
                                      ALU.subtract).then_inc(w_ready, 1)
                elif what == "stats":
                    src = source(st[1])
                    if st[1] == "first":
                        dve.wait_ge(x_in, 16 if half == "start" else 16 * (r.k + 2))
                    elif st[1] == "attn":
                        dve.wait_ge(x_updated, 2 * pass_of(r, "A") + 2)
                    else:
                        dve.wait_ge(x_c_ready, 2 * r.batch(half) + 2)
                    for i in range(T):
                        ins = dve.bn_stats(bn6[:, i, :], src[:, i, :])
                    link(ins)
                    met(dve)
                    for i in range(T):
                        ins = dve.bn_aggr(mean_var[:, i, :], bn6[:, i, :])
                    ins.then_inc(stats_done, 1)
                elif what == "norm":
                    src = source(st[1])
                    dve.wait_ge(stats_done, r.normed(st[1]) + 1)
                    dve.wait_ge(rstd_done, r.normed(st[1]) + 1)
                    if st[1] == "second":
                        dve.wait_ge(p_lo_done, FILLS * (r.batch(half) + 1))
                    elif st[1] == "first" and half == "B":
                        dve.wait_ge(part3_done, 6 * r.batch(half) + 6)
                    for i in range(T):
                        ins = dve.tensor_scalar(xn[:, i, :], src[:, i, :], mean_var[:, i, 0:1],
                                                rstd[:, i:i + 1], ALU.subtract, ALU.mult)
                    if st[1] == "attn":
                        link(ins)
                        link(dve.tensor_tensor(flat(x_b[:]), flat(x_b[:]), flat(xn), ALU.add))
                        for i in range(T):
                            ins = dve.tensor_scalar(xn[:, i, :], xn[:, i, :], rms_scale[:, i:i + 1], None,
                                                    ALU.mult)
                    ins.then_inc(xn_ready, 1)
                elif what == "transpose":
                    n = r.transposed(st[1])
                    hi, lo = xt_of(st[1])
                    for kb in range(KB):
                        dve.wait_ge(xt_hi_done, 2 * n + kb + 1)
                        if st[1] == "attn":
                            ins = dve.scalar_tensor_tensor(
                                out=lo[:, kb, :], in0=ps_t[:, kb, :], scalar=rms_col[:, kb:kb + 1],
                                in1=hi[:, kb, :].bitcast(F32), op0=ALU.mult, op1=ALU.subtract)
                        else:
                            ins = dve.tensor_tensor(lo[:, kb, :], ps_t[:, kb, :], hi[:, kb, :].bitcast(F32),
                                                    ALU.subtract)
                        ins.then_inc(xt_lo_done, 1)
                elif what == "route_a":
                    dve.wait_ge(xn_ready, r.normed(st[1]) + 1)
                    for i in range(T):
                        link(dve.tensor_tensor_reduce(junk, xn[:, i, :], w_diff[:, 0, :], 1.0, 0.0,
                                                      ALU.mult, ALU.add, dlogit[:, i:i + 1]))
                    dve.scalar_tensor_tensor(out=neg_abs[:], in0=dlogit[:], scalar=-1.0, in1=dlogit[:],
                                             op0=ALU.mult, op1=ALU.min).then_inc(dlogit_done, 1)
                elif what == "route_b":
                    coef = coef_a if st[1] == "first" else coef_b
                    dve.wait_ge(e_abs_done, r.routed(st[1]) + 1)
                    link(dve.tensor_scalar(prob[:], e_abs[:], 4.0, 4.0, ALU.mult, ALU.add))
                    dve.reciprocal(prob[:], prob[:]).then_inc(dve_link, 1)
                    link.n += 1
                    dve.wait_ge(dve_link, link.base + link.n)
                    dve.scalar_tensor_tensor(out=coef[:, 0, :], in0=dlogit[:], scalar=0.0, in1=prob[:],
                                             op0=ALU.is_ge, op1=ALU.mult)
                    link(dve.scalar_tensor_tensor(out=coef[:, 1, :], in0=dlogit[:], scalar=0.0, in1=prob[:],
                                                  op0=ALU.is_lt, op1=ALU.mult))
                elif what == "up":
                    u = r.unit(half) + st[1]
                    h = hid[:, st[1] % 2, :]
                    dve.wait_ge(tanh_done, u + 1)
                    dve.scalar_tensor_tensor(out=h, in0=h, scalar=1.0, in1=ps_g[:], op0=ALU.add,
                                             op1=ALU.mult).then_inc(gated, 1)
                    dve.wait_ge(gated, u + 1)
                    dve.wait_ge(u_done, u + 1)
                    dve.tensor_tensor(h, h, ps_u[:], ALU.mult).then_inc(h_done, 1)
                elif what == "x_update":
                    u, s = down_unit(half, r, st[1])
                    e = s // FB
                    of_a = (half == "A") == (st[1] >= 0)
                    coef = coef_a if of_a else coef_b
                    src = x_a if of_a else x_c
                    dst = (x_b if of_a else x_c) if e else src
                    dve.wait_ge(down_done, u + 1)
                    if e:
                        base = u - (UNITS - 1)
                        dve.wait_ge(x_updated, passes(half, r, st[1]) * 2 + 1)
                    for i in range(T):
                        ins = dve.scalar_tensor_tensor(out=dst[:, i, :], in0=ps_y[:, i, :],
                                                       scalar=coef[:, e, i:i + 1], in1=src[:, i, :],
                                                       op0=ALU.mult, op1=ALU.add)
                    ins.then_inc(x_updated, 1)
                elif what == "proj":
                    a, c = r.batch(half), st[1]
                    dve.wait_ge(part1_done, 6 * a + c + 1)
                    if c >= 2:
                        dve.wait_ge(part3_done, 6 * a + c - 1)
                    if c < 4:
                        ins = dve.scalar_tensor_tensor(out=rest[:, c % 2, :], in0=ps_r[:, c % 2, :],
                                                       scalar=1.0 if c % 2 else QSCALE,
                                                       in1=qk_parts[:, c, 0, :], op0=ALU.mult,
                                                       op1=ALU.subtract)
                    else:
                        j = 2 * (c - 4)
                        ins = dve.tensor_tensor(
                            rest[:, c % 2, :].rearrange("p (i h d) -> p i h d", i=2, h=H),
                            ps_r[:, c % 2, :].rearrange("p (i h d) -> p i h d", i=2, h=H),
                            v_parts[:, j:j + 2, :, 0:HD], ALU.subtract)
                    ins.then_inc(rest_done, 1)
                elif what == "proj_rest":
                    a, c = r.batch(half), st[1]
                    dve.wait_ge(part2_done, 6 * a + c + 1)
                    if c < 4:
                        ins = dve.tensor_tensor(qk_parts[:, c, 2, :], rest[:, c % 2, :],
                                                qk_parts[:, c, 1, :], ALU.subtract)
                    else:
                        j = 2 * (c - 4)
                        ins = dve.tensor_tensor(
                            v_parts[:, j:j + 2, :, 2 * HD:3 * HD],
                            rest[:, c % 2, :].rearrange("p (i h d) -> p i h d", i=2, h=H),
                            v_parts[:, j:j + 2, :, HD:2 * HD], ALU.subtract)
                    ins.then_inc(part3_done, 1)
                elif what == "scores":
                    a, f = r.batch(half), st[1]
                    dve.wait_ge(s_done, FILLS * a + f + 1)
                    met(dve)
                    for i, at in S_FILLS[f % 3]:
                        n = P * (i + 1)
                        s = ps_r[:, f % 2, at:at + n]
                        at_min = H * i + f // 3
                        ins = dve.tensor_tensor_reduce(s, s, mask[:, S - n:S], 1.0, HUGE, ALU.add, ALU.min,
                                                       row_min[:, at_min:at_min + 1])
                    ins.then_inc(max_done, 1)
                elif what == "row_max":
                    a = r.batch(half)
                    m = ps_m[0:T * H]
                    parts, left = max_parts[0:T * H], w_diff[0:T * H, 1, 0:P]
                    dve.wait_ge(mt_done, a + 1)
                    link(dve.tensor_scalar(parts[:, 0, :], m, -1.0, None, ALU.mult))
                    link(dve.scalar_tensor_tensor(out=left, in0=m, scalar=-1.0, in1=parts[:, 0, :],
                                                  op0=ALU.mult, op1=ALU.subtract))
                    link(dve.tensor_copy(parts[:, 1, :], left))
                    dve.tensor_tensor(parts[:, 2, :], left, parts[:, 1, :],
                                      ALU.subtract).then_inc(max_parts_done, 1)
                elif what == "p_split":
                    a, f = r.batch(half), st[1]
                    n = ST_WIDTH[f % 3]
                    dve.wait_ge(p_hi_done, FILLS * a + f + 1)
                    dve.tensor_tensor(p_lo[:, f % 3, 0:n], p_f32[:, f % 2, 0:n], p_hi[:, f % 3, 0:n],
                                      ALU.subtract).then_inc(p_lo_done, 1)
                elif what == "o_norm":
                    a, g = r.batch(half), st[1]
                    dve.wait_ge(o_copied, H * a + HG * (g + 1))
                    if g == 0 and not (r.fixed and r.k == 1):
                        dve.wait_ge(x_out, 16 * a)
                    o = x_c[:, :, HD * HG * g:HD * HG * (g + 1)].rearrange("p i (h d) -> p i h d", h=HG)
                    dve.tensor_tensor(o, o_raw[:, :, :, 0:HD], o_raw[:, :, :, HD:2 * HD], ALU.add)
                    link(dve.reciprocal(recip[:], o_raw[:, :, :, 3 * HD]))
                    link(dve.tensor_tensor(o, o, o_raw[:, :, :, 2 * HD:3 * HD], ALU.add))
                    dve.tensor_tensor(o, o, recip[:].unsqueeze(3).to_broadcast([P, T, HG, HD]),
                                      ALU.mult).then_inc(o_normed, 1)
                elif what == "out_proj":
                    a, g = r.batch(half), st[1]
                    dve.wait_ge(wo_done, 2 * a + g + 1)
                    dve.tensor_tensor(flat(x_c[:, 2 * g:2 * g + 2, :]), ps_r[:, g, :],
                                      flat(x_b[:, 2 * g:2 * g + 2, :]), ALU.add).then_inc(x_c_ready, 1)

            def passes(half, r, s):
                if half == "end":
                    return 15
                if s >= 0:
                    return pass_of(r, half)
                return pass_of(r, half) - 1 if not (half == "B" and r.first) else 0

            for st in start_stages:
                emit("start", Start(), st)
            run(dve, emit, link.enter)

        @block.tensor
        def _(pe):
            def three(out_ap, a, b, first, last, check=True):
                n = len(a)
                for i in range(n):
                    (a_hi, a_lo), (b_hi, b_lo) = a[i], b[i]
                    for j, (l, r) in enumerate(((a_hi, b_hi), (a_hi, b_lo), (a_lo, b_hi))):
                        ins = pe.matmul(out_ap, l, r, start=first and i == 0 and j == 0,
                                        stop=last and i == n - 1 and j == 2, skip_group_check=not check)
                return ins

            def emit(half, r, st):
                what = st[0]
                if what == "transpose":
                    n = r.transposed(st[1])
                    if st[1] == "o":
                        pe.wait_ge(o_normed, 2 * r.batch(half) + 2)
                        src = x_c
                    else:
                        pe.wait_ge(xn_ready, r.normed(st[1]) + 1)
                        src = xn
                    if half == "start":
                        pe.wait_ge(const_ready, 1)
                    else:
                        pe.wait_ge(xt_lo_done, 2 * n)
                    for kb in range(KB):
                        for i in range(T):
                            ins = pe.transpose(ps_t[:, kb, i * P:(i + 1) * P],
                                               src[:, i, kb * P:(kb + 1) * P], ident[:])
                        ins.then_inc(t_done, 1)
                elif what in ("gate", "up"):
                    s = st[1]
                    u = r.unit(half) + s
                    e, f = s // FB, s % FB
                    xh, xl = (xt_a_hi, xt_a_lo) if half == "A" else (xt_b_hi, xt_b_lo)
                    wh, wl, ps = (wg_hi, wg_lo, ps_g) if what == "gate" else (wu_hi, wu_lo, ps_u)
                    if half == "A" and r.first and f == 0:
                        pe.wait_ge(w_ready, (1 if what == "gate" else 2) + 3 * e)
                    if s == 0 and what == "gate":
                        if half == "A":
                            pe.wait_ge(xt_lo_done, 2 if r.first else 2 * (4 * r.k - 2) + 2)
                        else:
                            pe.wait_ge(xt_lo_done, 2 * r.transposed("second") + 2)
                    if not (half == "A" and r.first and s == 0):
                        pe.wait_ge(gated if what == "gate" else h_done, u)
                    cols = slice(f * P, (f + 1) * P)
                    three(ps[:], [(wh[:, e, kb, cols], wl[:, e, kb, cols]) for kb in range(KB)],
                          [(xh[:, kb, :], xl[:, kb, :]) for kb in range(KB)], True, True
                          ).then_inc(g_done if what == "gate" else u_done, 1)
                elif what == "down":
                    u, s = down_unit(half, r, st[1])
                    i = st[2]
                    e, f = s // FB, s % FB
                    if i == 0:
                        if half == "A" and r.first and f == 0:
                            pe.wait_ge(w_ready, 3 * (e + 1))
                        pe.wait_ge(h_lo_done, u + 1)
                        if f == 0:
                            if not (half == "A" and r.first and e == 0):
                                pe.wait_ge(x_updated, 2 * pass_of(r, half) + e)
                    cols = slice(i * P, (i + 1) * P)
                    ins = three(ps_y[:, i, :], [(h_hi[:, cols], h_lo[:, cols])],
                                [(wd_hi[:, e, f, :], wd_lo[:, e, f, :])], f == 0 and i % 2 == 0,
                                f == FB - 1, check=False)
                    if i == T - 1:
                        ins.then_inc(down_done, 1)
                elif what == "proj":
                    a, c = r.batch(half), st[1]
                    ps = ps_r[:, c % 2, :]
                    if c == 0:
                        pe.wait_ge(xt_lo_done, 2 * r.transposed("attn") + 2)
                        if r.first:
                            pe.wait_ge(w_ready, PIECES)
                    if c >= 2:
                        pe.wait_ge(rest_done, 6 * a + c - 1)
                    elif not r.first:
                        pe.wait_ge(x_c_ready, 2 * a + c - 1)
                    if c < 4:
                        at = (WK if c % 2 else WQ) + (c // 2) * P
                        ins = three(ps, [(wa_hi[:, kb, at:at + P], wa_lo[:, kb, at:at + P]) for kb in range(KB)],
                                    [(xt_a_hi[:, kb, :], xt_a_lo[:, kb, :]) for kb in range(KB)], True, True)
                    else:
                        for t in range(2):
                            i = 2 * (c - 4) + t
                            cols = slice(i * P, (i + 1) * P)
                            ins = three(ps[:, t * D:(t + 1) * D],
                                        [(xt_a_hi[:, kb, cols], xt_a_lo[:, kb, cols]) for kb in range(KB)],
                                        [(wa_hi[:, kb, WV:WV + D], wa_lo[:, kb, WV:WV + D]) for kb in range(KB)],
                                        True, True)
                    ins.then_inc(proj_done, 1)
                elif what == "scores":
                    a, f = r.batch(half), st[1]
                    h = f // 3
                    if f % (3 * HG) == 0:
                        pe.wait_ge(qk_loaded[h // HG], 192 * (a + 1))
                    if f >= 2:
                        pe.wait_ge(max_done, FILLS * a + f - 1)
                    else:
                        pe.wait_ge(rest_done, 6 * a + 5 + f)
                    for i, at in S_FILLS[f % 3]:
                        n = P * (i + 1)
                        ins = pe.matmul(ps_r[:, f % 2, at:at + n], qt[0:ROWS, h, i * P:n],
                                        kt[0:ROWS, h, 0:n], start=True, stop=True)
                    ins.then_inc(s_done, 1)
                elif what == "row_max":
                    a = r.batch(half)
                    pe.wait_ge(max_done, FILLS * (a + 1))
                    last = r.transposed("attn") if r.fixed and r.k == B - 1 else r.transposed("first")
                    pe.wait_ge(xt_lo_done, 2 * last + 2)
                    pe.transpose(ps_m, row_min[:], ident[:]).then_inc(mt_done, 1)
                elif what == "scores_t":
                    a, f = r.batch(half), st[1]
                    h = f // 3
                    if f == 0:
                        pe.wait_ge(max_in, 48 * (a + 1))
                        pe.wait_ge(ones_ready, 1)
                    if f >= 2:
                        pe.wait_ge(exp_done, FILLS * a + f - 1)
                    else:
                        pe.wait_ge(max_done, FILLS * a + FILLS - 1 + f)
                    for j, at in ST_FILLS[f % 3]:
                        n = S - P * j
                        ins = pe.matmul(ps_r[:, f % 2, at:at + n], kt[0:ROWS + 3, h, j * P:(j + 1) * P],
                                        qt[0:ROWS + 3, h, j * P:S], start=True, stop=True)
                    ins.then_inc(st_done, 1)
                elif what == "pv":
                    a, f = r.batch(half), st[1]
                    h = f // 3
                    pe.wait_ge(p_lo_done, FILLS * a + f + 1)
                    if f % 3 == 0:
                        pe.wait_ge(o_copied, H * a + h)
                    if f == 0:
                        pe.wait_ge(part3_done, 6 * a + 6)
                    for j, at in ST_FILLS[f % 3]:
                        for i in range(j, T):
                            for p in (p_hi, p_lo):
                                ins = pe.matmul(ps_o[:, i * VW:(i + 1) * VW],
                                                p[:, f % 3, at + (i - j) * P:at + (i - j + 1) * P],
                                                v_parts[:, j, h, :],
                                                start=(f % 3 == 0 and i == 0 and p is p_hi),
                                                stop=(f % 3 == 2), skip_group_check=True)
                    ins.then_inc(pv_done, 1)
                elif what == "out_proj":
                    a, g = r.batch(half), st[1]
                    if g == 0:
                        pe.wait_ge(xt_lo_done, 2 * r.transposed("o") + 2)
                    pe.wait_ge(exp_done, FILLS * a + FILLS - 1 + g)
                    for t in range(2):
                        i = 2 * g + t
                        cols = slice(i * P, (i + 1) * P)
                        ins = three(ps_r[:, g, t * D:(t + 1) * D],
                                    [(xt_b_hi[:, kb, cols], xt_b_lo[:, kb, cols]) for kb in range(KB)],
                                    [(wa_hi[:, kb, WO:WO + D], wa_lo[:, kb, WO:WO + D]) for kb in range(KB)],
                                    True, True)
                    ins.then_inc(wo_done, 1)

            for st in start_stages:
                emit("start", Start(), st)
            run(pe, emit)


def kernel(L0_attn_x, L0_attn_rms_w, L0_attn_Wq, L0_attn_Wk, L0_attn_Wv, L0_attn_Wo, L0_ffn_gate_w,
           L0_ffn_w_gate, L0_ffn_w_up, L0_ffn_w_down):
    import concourse.bacc as bacc
    import numpy as np
    from concourse.bass_utils import run_bass_kernel_spmd

    def rows(w):
        w = np.asarray(w)
        w = w.reshape(*w.shape[:-2], w.shape[-2] // P, P, w.shape[-1])
        return np.ascontiguousarray(np.moveaxis(w, -2, 0))

    attn = np.concatenate([np.asarray(w) for w in (L0_attn_Wq, L0_attn_Wk, L0_attn_Wv, L0_attn_Wo)], axis=1)
    arrays = {
        "x": np.ascontiguousarray(L0_attn_x),
        "rms_w": np.ascontiguousarray(np.asarray(L0_attn_rms_w).reshape(KB, P).T),
        "gate_w": np.ascontiguousarray(L0_ffn_gate_w),
        "w_gate": rows(np.swapaxes(np.asarray(L0_ffn_w_gate), 1, 2)),
        "w_up": rows(np.swapaxes(np.asarray(L0_ffn_w_up), 1, 2)),
        "w_down": rows(np.swapaxes(np.asarray(L0_ffn_w_down), 1, 2)),
        "w_attn": rows(attn),
    }
    nc = bacc.Bacc("TRN2", target_bir_lowering=False, num_devices=1)
    args = [nc.dram_tensor(n, a.shape, mybir.dt.from_np(a.dtype), kind="ExternalInput").ap()
            for n, a in arrays.items()]
    args.append(nc.dram_tensor("out", (B, S, D), F32, kind="ExternalOutput").ap())
    macaron(nc, *args)
    r = run_bass_kernel_spmd(nc, [arrays], core_ids=[0])
    return r.results[0]["out"]
```

```python
from contextlib import ExitStack

import concourse.bass as bass
from concourse import mybir

F32 = mybir.dt.float32
F32R = mybir.dt.float32r
BF16 = mybir.dt.bfloat16
F16 = mybir.dt.float16
ALU = mybir.AluOpType
ACT = mybir.ActivationFunctionType

P = 128
B, S, D = 8, 512, 256
E, FF = 2, 1024
H = 16
HD = D // H
T = S // P
KB = D // P
FB = FF // P
UNITS = E * FB
EPS = 1e-5
QSCALE = -1.0 / 16.0
HUGE = 3e38
TWO_ONES = 1.0 + 0x3F80 / 2**23
QPART = [0, 1, 2, 0, 1, 0]
KPART = [0, 0, 0, 1, 1, 2]
ROWS = HD * len(QPART)
VW = 3 * HD + 1
FILLS = 3 * H
GROUPS = 2
HG = H // GROUPS
OG = 4
WQ, WK, WV, WO = 0, D, 2 * D, 3 * D
PIECES = 3 * E + 1
STAGES = 4

S_FILLS = [[(3, 0)], [(2, 0), (0, 384)], [(1, 0)]]
ST_FILLS = [[(0, 0)], [(1, 0), (3, 384)], [(2, 0)]]
ST_WIDTH = [512, 512, 256]

DVE_LINKS = {"start": 8, "A0": 0, "A": 32, "B0": 13, "B": 13, "B7": 5}
POOL_LINKS = {"start": 6, "A0": 0, "A": 2, "B0": 4, "B": 4, "B7": 2}


def half_a(k, ffn, attend):
    plan = {}
    if attend:
        fills = []
        for f in range(FILLS + 3):
            now = []
            if f < FILLS:
                now += [("scores_t", f), ("exp", f), ("causal", f)]
            if 1 <= f < FILLS + 1:
                now += [("p_hi", f - 1)]
            if 2 <= f < FILLS + 2:
                now += [("p_lo", f - 2)]
            if f >= 3:
                now += [("pv", f - 3)]
                if (f - 3) % (3 * OG) == 3 * OG - 1:
                    now += [("o_norm", (f - 3) // (3 * OG))]
            fills.append(now)
        place(plan, A_SCORES, fills)
        put(plan, (12, 1), ("transpose", "o"))
        put(plan, (12, 4), ("out_proj", 0), ("out_proj", 1))
        put(plan, (13, 1), ("stats", "second"))
        put(plan, (14, 0), ("norm", "second"))
        put(plan, (14, 3), ("transpose", "second"))
        put(plan, (14, 4), ("route_a", "second"))
        put(plan, (15, 2), ("route_b", "second"))
    if ffn and isinstance(k, int) and k == 0:
        for n, s in ((2, 0), (3, 2), (4, 3), (5, 5), (6, 6)):
            put(plan, (s, 4), ("weights", n))
    return steps("A", k, ffn, plan)


def half_b(k, ffn, project, ahead):
    plan = {}
    if project:
        put(plan, (0, 4), ("stats", "attn"))
        put(plan, (2, 1), ("norm", "attn"))
        put(plan, (2, 3), ("transpose", "attn"))
        put(plan, (3, 0), ("residual", "attn"))
        proj = [[] for _ in range(8)]
        for c in range(6):
            proj[c].append(("proj", c))
            proj[c + 1].append(("proj_rest", c))
        proj[3].append(("qk_in", 0))
        proj[5].append(("qk_in", 1))
        place(plan, B_PROJ, proj)
        if ahead:
            put(plan, (3, 4), ("stats", "first"))
            put(plan, (5, 0), ("norm", "first"))
            put(plan, (5, 3), ("transpose", "first"))
            put(plan, (5, 4), ("route_a", "first"))
            put(plan, (6, 1), ("route_b", "first"))
        place(plan, B_SCORES, [[("scores", f)] for f in range(FILLS)])
        put(plan, (15, 4), ("row_max", 0))
    return steps("B", k, ffn, plan)


A_SCORES, B_PROJ, B_SCORES = (1, 3), (3, 2), (6, 0)
POINTS = 5


def put(plan, where, *stages):
    plan.setdefault(where, []).extend(stages)


def place(plan, start, groups):
    at = start[0] * POINTS + start[1]
    for n, group in enumerate(groups):
        where = min(at + n, UNITS * POINTS - 1)
        put(plan, (where // POINTS, where % POINTS), *group)


def steps(half, k, ffn, plan):
    out = []
    pending = not (isinstance(k, int) and (half, k) in (("A", 0), ("A", 1), ("B", B)))
    for s in range(UNITS):
        down = ffn if s else pending
        for kb in range(KB):
            if ffn:
                out.append(("gate", s, kb))
            if kb == 0:
                out.extend(plan.get((s, 0), []))
        for kb in range(KB):
            if ffn:
                out.append(("up", s, kb))
            out.extend(plan.get((s, 1 + kb), []))
        for i in range(T):
            if down:
                out.append(("down", s - 1, i))
            if i % 2:
                if down and i == T - 1 and s in (0, FB):
                    out.append(("x_update", s - 1))
                out.extend(plan.get((s, 3 + i // 2), []))
        if ffn:
            out.append(("h_split", s))
    return out


class Round:

    def __init__(self, k):
        self.k = k
        self.fixed = isinstance(k, int)
        self.first = self.fixed and k == 0
        self.last = self.fixed and k == B

    def unit(self, half):
        if half == "A":
            return 0 if self.first else 32 * self.k - 16
        return 240 if self.last else 16 if self.first else 32 * self.k

    def batch(self, half):
        return self.k - 1 if half == "A" else self.k

    def transposed(self, what):
        if what == "first":
            return 2 if self.first else 4 * self.k + 2
        if what == "attn":
            return 1 if self.first else 4 * self.k + 1
        short = 1 if self.last else 0
        return 4 * self.k - 1 - short if what == "o" else 4 * self.k - short

    def normed(self, what):
        if what == "first":
            return 2 if self.first else 3 * self.k + 2
        if what == "attn":
            return 1 if self.first else 3 * self.k + 1
        return 3 * self.k - (1 if self.last else 0)

    def routed(self, what):
        if what == "first":
            return 1 if self.first else 2 * self.k + 1
        return 2 * self.k - (1 if self.last else 0)


class Start(Round):

    def __init__(self):
        Round.__init__(self, 0)

    def transposed(self, what):
        return 0

    def normed(self, what):
        return 0

    def routed(self, what):
        return 0


class Links:

    def __init__(self, eng, sem, per_part):
        self.eng, self.sem, self.per = eng, sem, per_part
        self.base, self.n, self.part = 0, 0, "start"

    def __call__(self, ins):
        self.n += 1
        ins.then_inc(self.sem, 1)
        self.eng.wait_ge(self.sem, self.base + self.n)

    def enter(self, part, k):
        assert self.n == self.per[self.part], (self.part, self.n)
        p = self.per
        before = p["start"]
        if part != "A0":
            before = before + p["A0"]
            if part != "B0":
                before = before + p["B0"] + (k - 1) * (p["A"] + p["B"])
                if part in ("B", "B7"):
                    before = before + p["A"]
        if part == "A" and isinstance(k, int) and k == B:
            before = before - p["B"] + p["B7"]
        self.base, self.n, self.part = before, 0, part


def macaron(nc, x, rms_w, gate_w, w_gate, w_up, w_down, w_attn, out):
    with ExitStack() as ctx:
        def sb(name, shape, dt):
            return ctx.enter_context(nc.sbuf_tensor(name, shape, dt))

        def sem(name):
            return ctx.enter_context(nc.semaphore(name))

        wg_hi = sb("wg_hi", [P, E, KB, FF], F32R)
        wg_lo = sb("wg_lo", [P, E, KB, FF], F32R)
        wu_hi = sb("wu_hi", [P, E, KB, FF], F32R)
        wu_lo = sb("wu_lo", [P, E, KB, FF], F32R)
        wd_hi = sb("wd_hi", [P, E, FB, D], F32R)
        wd_lo = sb("wd_lo", [P, E, FB, D], F32R)
        wa_hi = sb("wa_hi", [P, KB, 4 * D], F32R)
        wa_lo = sb("wa_lo", [P, KB, 4 * D], F32R)
        x_a = sb("x_a", [P, T, D], F32)
        x_b = sb("x_b", [P, T, D], F32)
        x_c = sb("x_c", [P, T, D], F32)
        xt_a_hi = sb("xt_a_hi", [P, KB, S], F32R)
        xt_a_lo = sb("xt_a_lo", [P, KB, S], F32R)
        xt_b_hi = sb("xt_b_hi", [P, KB, S], F32R)
        xt_b_lo = sb("xt_b_lo", [P, KB, S], F32R)
        hid = sb("hid", [P, 2, S], F32)
        h_hi = sb("h_hi", [P, S], F32R)
        h_lo = sb("h_lo", [P, S], F32R)
        qt = sb("qt", [P, H, S], BF16)
        kt = sb("kt", [P, H, S], BF16)
        v_parts = sb("v_parts", [P, T, H, VW], BF16)
        p_words, split_words, o_words = 3 * S, 4 * S, T * OG * VW
        area = sb("area", [P, p_words + split_words + o_words], F32)
        p_f32 = area[:, 0:p_words].rearrange("p (r n) -> p r n", r=3)
        p_f16 = area[:, p_words:p_words + split_words].bitcast(F16)
        p_hi = p_f16[:, 0:4 * S].rearrange("p (r n) -> p r n", r=4)
        p_lo = p_f16[:, 4 * S:8 * S].rearrange("p (r n) -> p r n", r=4)
        o_raw = area[:, p_words + split_words:].rearrange("p (i h c) -> p i h c", i=T, h=OG)
        xn = area[:, 0:T * D].rearrange("p (i d) -> p i d", i=T)
        rest = area[:, 0:2 * S].rearrange("p (r n) -> p r n", r=2)
        max_parts = area[:, 0:3 * P // 2].bitcast(BF16).rearrange("p (r n) -> p r n", r=3)
        max_rest = area[:, 2 * P:3 * P]
        qk_parts = area[:, 2 * S:2 * S + 6 * S].bitcast(BF16).rearrange("p (c r n) -> p c r n", c=4, r=3)
        ident = sb("ident", [P, P], F32)
        mask = sb("mask", [P, S], BF16)
        w_diff = sb("w_diff", [P, D], F32)
        rms_col = sb("rms_col", [P, KB], F32)
        minus_half = sb("minus_half", [P, 2, T], F32)
        bn6 = sb("bn6", [P, T, 6], F32)
        mean_var = sb("mean_var", [P, T, 2], F32)
        scales = sb("scales", [P, 2, T], F32)
        shifts = sb("shifts", [P, 2, T], F32)
        minus_mean = sb("minus_mean", [P, T], F32)
        res_scale = sb("res_scale", [P, T], F32)
        tmp_pool = sb("tmp_pool", [P, 2, T], F32)
        dlogit = sb("dlogit", [P, T], F32)
        neg_abs = sb("neg_abs", [P, T], F32)
        e_abs = sb("e_abs", [P, T], F32)
        prob = sb("prob", [P, T], F32)
        coef_a = sb("coef_a", [P, E, T], F32)
        coef_b = sb("coef_b", [P, E, T], F32)
        row_min = sb("row_min", [P, P], F32)
        junk = sb("junk", [P, D], BF16)
        recip = sb("recip", [P, T, OG], F32)

        ps_g = ctx.enter_context(nc.psum_tensor("ps_g", [P, S], F32))
        ps_u = ctx.enter_context(nc.psum_tensor("ps_u", [P, S], F32))
        ps_y = ctx.enter_context(nc.psum_tensor("ps_y", [P, T, D], F32))
        ps_t = ctx.enter_context(nc.psum_tensor("ps_t", [P, KB, S], F32))
        ps_r = ctx.enter_context(nc.psum_tensor("ps_r", [P, 2, S], F32))
        ps_o = [ps_t[:, h, 0:T * VW] for h in range(2)]
        ps_m = ps_t[:, 0, 0:P]

        qk_scratch = nc.dram_tensor("qk_scratch", [4, 3, HG, HD, S], BF16, kind="Internal").ap()
        max_scratch = nc.dram_tensor("max_scratch", [3, T, H, P], BF16, kind="Internal").ap()

        w_in = [sem(f"w_in{n}") for n in range(PIECES)]
        small_in, x_in, x_out = sem("small_in"), sem("x_in"), sem("x_out")
        max_saved, max_in = sem("max_saved"), sem("max_in")
        qk_saved = [sem(f"qk_saved{g}") for g in range(GROUPS)]
        qk_loaded = [sem(f"qk_loaded{g}") for g in range(GROUPS)]
        const_ready, ones_ready, diff_ready = sem("const_ready"), sem("ones_ready"), sem("diff_ready")
        w_hi_done, w_ready = sem("w_hi_done"), sem("w_ready")
        stats_done, rstd_done, xn_ready = sem("stats_done"), sem("rstd_done"), sem("xn_ready")
        t_done, xt_hi_done, xt_lo_done = sem("t_done"), sem("xt_hi_done"), sem("xt_lo_done")
        dlogit_done, e_abs_done = sem("dlogit_done"), sem("e_abs_done")
        g_done, u_done, tanh_done = sem("g_done"), sem("u_done"), sem("tanh_done")
        gated, h_done = sem("gated"), sem("h_done")
        h_hi_done, h_lo_done = sem("h_hi_done"), sem("h_lo_done")
        down_done, x_updated = sem("down_done"), sem("x_updated")
        proj_done, part1_done, rest_done, part2_done, part3_done = (
            sem("proj_done"), sem("part1_done"), sem("rest_done"), sem("part2_done"), sem("part3_done"))
        s_done, max_done, mt_done, max_parts_done = (
            sem("s_done"), sem("max_done"), sem("mt_done"), sem("max_parts_done"))
        st_done, exp_done, causal_done = sem("st_done"), sem("exp_done"), sem("causal_done")
        p_hi_done, p_lo_done, pv_done = sem("p_hi_done"), sem("p_lo_done"), sem("pv_done")
        o_copied, o_normed, wo_done, x_c_ready = sem("o_copied"), sem("o_normed"), sem("wo_done"), sem("x_c_ready")
        dve_link, pool_link = sem("dve_link"), sem("pool_link")
        met_waits = {nc.vector: sem("dve_met"), nc.gpsimd: sem("pool_met"), nc.sync: sem("sp_met")}

        stage = [
            (qt if n < 2 else kt)[:, 8 * (n % 2):8 * (n % 2) + 8, :].bitcast(F32).rearrange("p h n -> p (h n)")
            for n in range(STAGES)
        ]
        raw = [w for e in range(E) for w in (w_gate[:, e], w_up[:, e], w_down[:, e])] + [w_attn]
        split = [(hi[:, e], lo[:, e]) for e in range(E)
                 for hi, lo in ((wg_hi, wg_lo), (wu_hi, wu_lo), (wd_hi, wd_lo))] + [(wa_hi[:], wa_lo[:])]

        def flat(ap):
            return ap.rearrange("p a b -> p (a b)")

        def xt_of(what):
            return (xt_a_hi, xt_a_lo) if what in ("first", "attn") else (xt_b_hi, xt_b_lo)

        def source(what):
            return {"first": x_a, "attn": x_b, "second": x_c}[what]

        def diag(ap):
            return ap.rearrange("p (a b) -> p a b", b=P)[:, 0:4:3, :]

        block = ctx.enter_context(nc.Block())

        def run(eng, emit, enter=None):
            def part(name, half, r, stages):
                if enter:
                    enter(name, r.k)
                for st in stages:
                    emit(half, r, st)

            first = Round(0)
            part("A0", "A", first, half_a(0, True, False))
            part("B0", "B", first, half_b(0, False, True, True))
            r = Round(1)
            part("A", "A", r, half_a(1, True, True))
            part("B", "B", r, half_b(1, True, True, True))
            with eng.Fori(2, B - 1) as k:
                r = Round(k)
                part("A", "A", r, half_a(k, True, True))
                part("B", "B", r, half_b(k, True, True, True))
            r = Round(B - 1)
            part("A", "A", r, half_a(B - 1, True, True))
            part("B7", "B", r, half_b(B - 1, True, True, False))
            r = Round(B)
            part("A", "A", r, half_a(B, False, True))
            for st in half_b(B, True, False, False):
                emit("B", r, st)
            for i in range(T):
                emit("end", r, ("down", UNITS - 1, i))
            emit("end", r, ("x_update", UNITS - 1))

        start_stages = [("weights", 0), ("stats", "first"), ("norm", "first"), ("transpose", "first"),
                        ("weights", 1), ("route_a", "first"), ("route_b", "first")]

        def pass_of(r, half):
            if half == "A":
                return 0 if r.first else 2 * r.k - 1
            return 15 if r.last else 2 * r.k

        def met(eng):
            eng.sem_inc(met_waits[eng], 1)

        def down_unit(half, r, s):
            base = r.unit("B") if half == "end" else r.unit(half)
            return base + s, s % UNITS

        @block.sync
        def _(sp):
            def batch_view(ap, n):
                return ap[bass.ds(n, 1)].rearrange("o (i p) d -> p (o i) d", p=P)

            sp.dma_start(x_a[:], batch_view(x, 0)).then_inc(x_in, 16)
            sp.dma_start(x_c[:, 0:E, :], gate_w.partition_broadcast(P)).then_inc(small_in, 16)
            sp.dma_start(rms_col[:], rms_w).then_inc(small_in, 16)
            for n in range(PIECES):
                if n >= STAGES:
                    sp.wait_ge(w_ready, n - STAGES + 1)
                sp.dma_start(stage[n % STAGES], flat(raw[n])).then_inc(w_in[n], 16)

            def emit(half, r, st):
                a = r.batch(half) if half != "end" else None
                if st[0] == "x_update":
                    u, s = down_unit(half, r, st[1])
                    if s != UNITS - 1:
                        return
                    if half == "B":
                        if not (r.last or r.fixed and r.k == B - 1):
                            sp.wait_ge(x_updated, 2 * pass_of(r, "A") + 2)
                            met(sp)
                            sp.dma_start(x_a[:], batch_view(x, r.k + 1)).then_inc(x_in, 16)
                    else:
                        done = 15 if half == "end" else None
                        n = B - 1 if half == "end" else r.k - 2
                        if half == "end":
                            sp.wait_ge(x_updated, 2 * (done + 1))
                        else:
                            sp.wait_ge(x_updated, 2 * (2 * r.k - 2) + 2)
                            met(sp)
                        sp.dma_start(batch_view(out, n), x_c[:]).then_inc(x_out, 16)
                elif st[0] == "proj_rest" and st[1] < 4:
                    c = st[1]
                    sp.wait_ge(part3_done, 6 * a + c + 1)
                    sp.dma_start(qk_scratch[c].rearrange("r h d t -> (h d) r t"),
                                 qk_parts[:, c]).then_inc(qk_saved[c // 2], 16)
                elif st[0] == "qk_in":
                    g = st[1]
                    sp.wait_ge(qk_saved[g], 32 * (a + 1))
                    met(sp)
                    if g == 0:
                        if r.first:
                            sp.wait_ge(w_ready, PIECES)
                        else:
                            sp.wait_ge(st_done, FILLS * a)
                    for n in range(len(QPART)):
                        rows = slice(HD * n, HD * n + HD)
                        heads = slice(HG * g, HG * g + HG)
                        sp.dma_start(qt[rows, heads, :], qk_scratch[2 * g, QPART[n]].rearrange(
                            "h d t -> d h t")).then_inc(qk_loaded[g], 16)
                        sp.dma_start(kt[rows, heads, :], qk_scratch[2 * g + 1, KPART[n]].rearrange(
                            "h d t -> d h t")).then_inc(qk_loaded[g], 16)
                elif st[0] == "row_max":
                    sp.wait_ge(max_parts_done, a + 1)
                    sp.dma_start(max_scratch.rearrange("r i h s -> (i h) r s"),
                                 max_parts[0:T * H]).then_inc(max_saved, 16)
                    sp.wait_ge(max_saved, 16 * (a + 1))
                    for n in range(3):
                        sp.dma_start(qt[ROWS + n:ROWS + n + 1].rearrange("o h (i s) -> o h i s", i=T),
                                     max_scratch[n:n + 1].rearrange("o i h s -> o h i s")
                                     ).then_inc(max_in, 16)

            run(sp, emit)
            sp.wait_ge(x_out, 16 * B)

        @block.gpsimd
        def _(pool):
            link = Links(pool, pool_link, POOL_LINKS)
            link(pool.memset(ident[:], 0.0))
            link(pool.affine_select(out=ident[:], in_=ident[:], compare_op=ALU.not_equal, fill=1.0,
                                    base=0, pattern=[[-1, P]], channel_multiplier=1))
            link(pool.memset(mask[:], 0.0))
            link(pool.affine_select(out=mask[:, S - P:S], in_=mask[:, S - P:S], compare_op=ALU.is_ge,
                                    fill=HUGE, base=0, pattern=[[-1, P]], channel_multiplier=1))
            pool.memset(minus_half[:], -0.5)
            pool.memset(v_parts[:], 1.0)
            pool.memset(row_min[:], 0.0).then_inc(const_ready, 1)
            pool.wait_ge(const_ready, 1)

            def emit(half, r, st):
                if st[0] == "stats":
                    n = r.normed(st[1])
                    pool.wait_ge(stats_done, n + 1)
                    met(pool)
                    mean, var = mean_var[:, :, 0], mean_var[:, :, 1]
                    pool.tensor_scalar(tmp_pool[:, 0, :], var, EPS, None, ALU.add)
                    pool.tensor_scalar(tmp_pool[:, 1, :], var, 1.0 + EPS, EPS * EPS, ALU.mult, ALU.add)
                    link(pool.tensor_scalar(minus_mean[:], mean, -1.0, None, ALU.mult))
                    link(pool.tensor_tensor(scales[:], tmp_pool[:], minus_half[:], ALU.pow))
                    ins = pool.tensor_tensor(shifts[:], scales[:],
                                             minus_mean[:].unsqueeze(1).to_broadcast([P, 2, T]), ALU.mult)
                    if st[1] == "attn":
                        ins = pool.tensor_scalar(res_scale[:], scales[:, 0, :], 1.0, None, ALU.add)
                    ins.then_inc(rstd_done, 1)
                elif st[0] == "weights" and st[1] == PIECES - 1:
                    pool.wait_ge(w_ready, PIECES)
                    pool.wait_ge(h_lo_done, 12)
                    pool.memset(kt[ROWS:ROWS + 3].bitcast(F32), TWO_ONES).then_inc(ones_ready, 1)
                    pool.wait_ge(ones_ready, 1)
                elif st[0] == "h_split":
                    u = r.unit(half) + st[1]
                    pool.wait_ge(h_hi_done, u + 1)
                    for c in (slice(0, S // 2), slice(S // 2, S)):
                        pool.tensor_tensor(h_lo[:, c], hid[:, st[1] % 2, c], h_hi[:, c].bitcast(F32),
                                           ALU.subtract).then_inc(h_lo_done, 1)
                elif st[0] == "causal":
                    f = st[1]
                    pool.wait_ge(exp_done, FILLS * r.batch(half) + f + 1)
                    met(pool)
                    p = p_f32[:, f % 3, :]
                    p = diag(p) if f % 3 == 1 else p[:, 0:P]
                    pool.affine_select(out=p, in_=p, compare_op=ALU.is_ge, fill=0.0, base=0,
                                       pattern=[[0, 2], [1, P]] if f % 3 == 1 else [[1, P]],
                                       channel_multiplier=-1).then_inc(causal_done, 1)

            for st in start_stages:
                emit("start", Start(), st)
            run(pool, emit, link.enter)

        @block.scalar
        def _(act):
            def emit(half, r, st):
                what = st[0]
                if what == "weights":
                    n = st[1]
                    act.wait_ge(w_in[n], 16)
                    act.activation(flat(split[n][0]), stage[n % STAGES], ACT.Copy).then_inc(w_hi_done, 1)
                elif what == "norm":
                    n = r.normed(st[1])
                    act.wait_ge(rstd_done, n + 1)
                    if st[1] == "second":
                        act.wait_ge(p_lo_done, FILLS * (r.batch(half) + 1))
                    elif st[1] == "first" and half == "B":
                        act.wait_ge(part3_done, 6 * r.batch(half) + 6)
                    both = 1 if st[1] == "attn" else 0
                    for i in range(T):
                        ins = act.activation(xn[:, i, :], source(st[1])[:, i, :], ACT.Identity,
                                             bias=shifts[:, both, i:i + 1], scale=scales[:, both, i:i + 1])
                    ins.then_inc(xn_ready, 1)
                elif what == "transpose":
                    n = r.transposed(st[1])
                    if half == "start" or r.first and st[1] == "attn":
                        act.wait_ge(small_in, 32)
                    for kb in range(KB):
                        act.wait_ge(t_done, 2 * n + kb + 1)
                        scale = rms_col[:, kb:kb + 1] if st[1] == "attn" else 1.0
                        act.activation(xt_of(st[1])[0][:, kb, :], ps_t[:, kb, :], ACT.Copy,
                                       scale=scale).then_inc(xt_hi_done, 1)
                elif what == "route_a":
                    act.wait_ge(dlogit_done, r.routed(st[1]) + 1)
                    act.activation(e_abs[:], neg_abs[:], ACT.Exp).then_inc(e_abs_done, 1)
                elif what == "gate" and st[2] == KB - 1:
                    u = r.unit(half) + st[1]
                    act.wait_ge(g_done, u + 1)
                    if not (r.first and half == "A" and st[1] < 2):
                        act.wait_ge(h_lo_done, 2 * u - 2)
                    act.activation(hid[:, st[1] % 2, :], ps_g[:], ACT.Tanh, scale=0.5).then_inc(tanh_done, 1)
                elif what == "h_split":
                    u = r.unit(half) + st[1]
                    act.wait_ge(h_done, u + 1)
                    act.wait_ge(down_done, u)
                    act.activation(h_hi[:], hid[:, st[1] % 2, :], ACT.Copy).then_inc(h_hi_done, 1)
                elif what == "proj":
                    a, c = r.batch(half), st[1]
                    act.wait_ge(proj_done, 6 * a + c + 1)
                    if c < 4:
                        act.activation(qk_parts[:, c, 0, :], ps_r[:, c % 2, :], ACT.Copy,
                                       scale=1.0 if c % 2 else QSCALE).then_inc(part1_done, 1)
                    else:
                        act.activation(v_parts[:, 2 * (c - 4):2 * (c - 4) + 2, :, 0:HD],
                                       ps_r[:, c % 2, :].rearrange("p (i h d) -> p i h d", i=2, h=H),
                                       ACT.Copy).then_inc(part1_done, 1)
                elif what == "proj_rest":
                    a, c = r.batch(half), st[1]
                    act.wait_ge(rest_done, 6 * a + c + 1)
                    if c < 4:
                        act.activation(qk_parts[:, c, 1, :], rest[:, c % 2, :], ACT.Copy).then_inc(part2_done, 1)
                    else:
                        act.activation(v_parts[:, 2 * (c - 4):2 * (c - 4) + 2, :, HD:2 * HD],
                                       rest[:, c % 2, :].rearrange("p (i h d) -> p i h d", i=2, h=H),
                                       ACT.Copy).then_inc(part2_done, 1)
                elif what == "exp":
                    a, f = r.batch(half), st[1]
                    act.wait_ge(st_done, FILLS * a + f + 1)
                    if f >= 3 or not (r.fixed and r.k == 1):
                        act.wait_ge(p_lo_done, FILLS * a + f - 2)
                    n = ST_WIDTH[f % 3]
                    act.activation(p_f32[:, f % 3, 0:n], ps_r[:, f % 2, 0:n], ACT.Exp,
                                   scale=-1.0).then_inc(exp_done, 1)
                elif what == "p_hi" and st[1] % 3:
                    a, f = r.batch(half), st[1]
                    act.wait_ge(causal_done, FILLS * a + f + 1)
                    if f >= 4 or not (r.fixed and r.k == 1):
                        act.wait_ge(pv_done, FILLS * a + f - 3)
                    n = ST_WIDTH[f % 3]
                    act.activation(p_hi[:, f % 4, 0:n], p_f32[:, f % 3, 0:n], ACT.Copy).then_inc(p_hi_done, 1)
                elif what == "pv" and st[1] % 3 == 2:
                    a, h = r.batch(half), st[1] // 3
                    act.wait_ge(pv_done, FILLS * a + 3 * h + 3)
                    if h % OG == 0:
                        act.wait_ge(o_normed, H // OG * a + h // OG)
                    act.activation(o_raw[:, :, h % OG, :], ps_o[h % 2].rearrange("p (i c) -> p i c", i=T),
                                   ACT.Copy).then_inc(o_copied, 1)

            for st in start_stages:
                emit("start", Start(), st)
            run(act, emit)

        @block.vector
        def _(dve):
            link = Links(dve, dve_link, DVE_LINKS)
            dve.wait_ge(small_in, 32)
            dve.tensor_tensor(w_diff[:], x_c[:, 0, :], x_c[:, 1, :], ALU.subtract).then_inc(diff_ready, 1)
            dve.wait_ge(diff_ready, 1)

            def emit(half, r, st):
                what = st[0]
                if what == "weights":
                    n = st[1]
                    dve.wait_ge(w_hi_done, n + 1)
                    dve.tensor_tensor(flat(split[n][1]), stage[n % STAGES], flat(split[n][0]).bitcast(F32),
                                      ALU.subtract).then_inc(w_ready, 1)
                elif what == "stats":
                    src = source(st[1])
                    if st[1] == "first":
                        dve.wait_ge(x_in, 16 if half == "start" else 16 * (r.k + 2))
                    elif st[1] == "attn":
                        dve.wait_ge(x_updated, 2 * pass_of(r, "A") + 2)
                    else:
                        dve.wait_ge(x_c_ready, 2 * r.batch(half) + 2)
                    for i in range(T):
                        ins = dve.bn_stats(bn6[:, i, :], src[:, i, :])
                    link(ins)
                    met(dve)
                    for i in range(T):
                        ins = dve.bn_aggr(mean_var[:, i, :], bn6[:, i, :])
                    ins.then_inc(stats_done, 1)
                elif what == "residual":
                    dve.wait_ge(xn_ready, r.normed(st[1]) + 1)
                    for i in range(T):
                        ins = dve.tensor_scalar(x_b[:, i, :], x_b[:, i, :], res_scale[:, i:i + 1],
                                                shifts[:, 0, i:i + 1], ALU.mult, ALU.add)
                    link(ins)
                elif what == "transpose":
                    n = r.transposed(st[1])
                    hi, lo = xt_of(st[1])
                    for kb in range(KB):
                        dve.wait_ge(xt_hi_done, 2 * n + kb + 1)
                        if st[1] == "attn":
                            ins = dve.scalar_tensor_tensor(
                                out=lo[:, kb, :], in0=ps_t[:, kb, :], scalar=rms_col[:, kb:kb + 1],
                                in1=hi[:, kb, :].bitcast(F32), op0=ALU.mult, op1=ALU.subtract)
                        else:
                            ins = dve.tensor_tensor(lo[:, kb, :], ps_t[:, kb, :], hi[:, kb, :].bitcast(F32),
                                                    ALU.subtract)
                        ins.then_inc(xt_lo_done, 1)
                elif what == "route_a":
                    dve.wait_ge(xn_ready, r.normed(st[1]) + 1)
                    for i in range(T):
                        link(dve.tensor_tensor_reduce(junk[:], xn[:, i, :], w_diff[:], 1.0, 0.0,
                                                      ALU.mult, ALU.add, dlogit[:, i:i + 1]))
                    dve.scalar_tensor_tensor(out=neg_abs[:], in0=dlogit[:], scalar=-1.0, in1=dlogit[:],
                                             op0=ALU.mult, op1=ALU.min).then_inc(dlogit_done, 1)
                elif what == "route_b":
                    coef = coef_a if st[1] == "first" else coef_b
                    dve.wait_ge(e_abs_done, r.routed(st[1]) + 1)
                    link(dve.tensor_scalar(prob[:], e_abs[:], 4.0, 4.0, ALU.mult, ALU.add))
                    dve.reciprocal(prob[:], prob[:]).then_inc(dve_link, 1)
                    link.n += 1
                    dve.wait_ge(dve_link, link.base + link.n)
                    dve.scalar_tensor_tensor(out=coef[:, 0, :], in0=dlogit[:], scalar=0.0, in1=prob[:],
                                             op0=ALU.is_ge, op1=ALU.mult)
                    link(dve.scalar_tensor_tensor(out=coef[:, 1, :], in0=dlogit[:], scalar=0.0, in1=prob[:],
                                                  op0=ALU.is_lt, op1=ALU.mult))
                elif what == "up" and st[2] == KB - 1:
                    u = r.unit(half) + st[1]
                    h = hid[:, st[1] % 2, :]
                    dve.wait_ge(tanh_done, u + 1)
                    dve.scalar_tensor_tensor(out=h, in0=h, scalar=1.0, in1=ps_g[:], op0=ALU.add,
                                             op1=ALU.mult).then_inc(gated, 1)
                    dve.wait_ge(gated, u + 1)
                    dve.wait_ge(u_done, u + 1)
                    dve.tensor_tensor(h, h, ps_u[:], ALU.mult).then_inc(h_done, 1)
                elif what == "x_update":
                    u, s = down_unit(half, r, st[1])
                    e = s // FB
                    of_a = (half == "A") == (st[1] >= 0)
                    coef = coef_a if of_a else coef_b
                    src = x_a if of_a else x_c
                    dst = (x_b if of_a else x_c) if e else src
                    dve.wait_ge(down_done, u + 1)
                    if e:
                        base = u - (UNITS - 1)
                        dve.wait_ge(x_updated, passes(half, r, st[1]) * 2 + 1)
                    for i in range(T):
                        ins = dve.scalar_tensor_tensor(out=dst[:, i, :], in0=ps_y[:, i, :],
                                                       scalar=coef[:, e, i:i + 1], in1=src[:, i, :],
                                                       op0=ALU.mult, op1=ALU.add)
                    ins.then_inc(x_updated, 1)
                elif what == "proj":
                    a, c = r.batch(half), st[1]
                    dve.wait_ge(part1_done, 6 * a + c + 1)
                    if c >= 2:
                        dve.wait_ge(part3_done, 6 * a + c - 1)
                    if c < 4:
                        ins = dve.scalar_tensor_tensor(out=rest[:, c % 2, :], in0=ps_r[:, c % 2, :],
                                                       scalar=1.0 if c % 2 else QSCALE,
                                                       in1=qk_parts[:, c, 0, :], op0=ALU.mult,
                                                       op1=ALU.subtract)
                    else:
                        j = 2 * (c - 4)
                        ins = dve.tensor_tensor(
                            rest[:, c % 2, :].rearrange("p (i h d) -> p i h d", i=2, h=H),
                            ps_r[:, c % 2, :].rearrange("p (i h d) -> p i h d", i=2, h=H),
                            v_parts[:, j:j + 2, :, 0:HD], ALU.subtract)
                    ins.then_inc(rest_done, 1)
                elif what == "proj_rest":
                    a, c = r.batch(half), st[1]
                    dve.wait_ge(part2_done, 6 * a + c + 1)
                    if c < 4:
                        ins = dve.tensor_tensor(qk_parts[:, c, 2, :], rest[:, c % 2, :],
                                                qk_parts[:, c, 1, :], ALU.subtract)
                    else:
                        j = 2 * (c - 4)
                        ins = dve.tensor_tensor(
                            v_parts[:, j:j + 2, :, 2 * HD:3 * HD],
                            rest[:, c % 2, :].rearrange("p (i h d) -> p i h d", i=2, h=H),
                            v_parts[:, j:j + 2, :, HD:2 * HD], ALU.subtract)
                    ins.then_inc(part3_done, 1)
                elif what == "scores":
                    a, f = r.batch(half), st[1]
                    dve.wait_ge(s_done, FILLS * a + f + 1)
                    met(dve)
                    for i, at in S_FILLS[f % 3]:
                        n = P * (i + 1)
                        s = ps_r[:, f % 2, at:at + n]
                        at_min = H * i + f // 3
                        ins = dve.tensor_tensor_reduce(s, s, mask[:, S - n:S], 1.0, HUGE, ALU.add, ALU.min,
                                                       row_min[:, at_min:at_min + 1])
                    ins.then_inc(max_done, 1)
                elif what == "row_max":
                    a = r.batch(half)
                    m = ps_m[0:T * H]
                    parts, left = max_parts[0:T * H], max_rest[0:T * H]
                    dve.wait_ge(mt_done, a + 1)
                    link(dve.tensor_scalar(parts[:, 0, :], m, -1.0, None, ALU.mult))
                    link(dve.scalar_tensor_tensor(out=left, in0=m, scalar=-1.0, in1=parts[:, 0, :],
                                                  op0=ALU.mult, op1=ALU.subtract))
                    link(dve.tensor_copy(parts[:, 1, :], left))
                    dve.tensor_tensor(parts[:, 2, :], left, parts[:, 1, :],
                                      ALU.subtract).then_inc(max_parts_done, 1)
                elif what == "p_lo":
                    a, f = r.batch(half), st[1]
                    n = ST_WIDTH[f % 3]
                    if f % 3:
                        dve.wait_ge(p_hi_done, 2 * H * a + 2 * (f // 3) + f % 3)
                    else:
                        dve.wait_ge(causal_done, FILLS * a + f + 1)
                        if f >= 4 or not (r.fixed and r.k == 1):
                            dve.wait_ge(pv_done, FILLS * a + f - 3)
                        link(dve.tensor_copy(p_hi[:, f % 4, 0:n], p_f32[:, f % 3, 0:n]))
                    dve.tensor_tensor(p_lo[:, f % 4, 0:n], p_f32[:, f % 3, 0:n], p_hi[:, f % 4, 0:n],
                                      ALU.subtract).then_inc(p_lo_done, 1)
                elif what == "o_norm":
                    a, g = r.batch(half), st[1]
                    dve.wait_ge(o_copied, H * a + OG * (g + 1))
                    if g == 0 and not (r.fixed and r.k == 1):
                        dve.wait_ge(x_out, 16 * a)
                    o = x_c[:, :, HD * OG * g:HD * OG * (g + 1)].rearrange("p i (h d) -> p i h d", h=OG)
                    dve.tensor_tensor(o, o_raw[:, :, :, 0:HD], o_raw[:, :, :, HD:2 * HD], ALU.add)
                    link(dve.reciprocal(recip[:], o_raw[:, :, :, 3 * HD]))
                    link(dve.tensor_tensor(o, o, o_raw[:, :, :, 2 * HD:3 * HD], ALU.add))
                    dve.tensor_tensor(o, o, recip[:].unsqueeze(3).to_broadcast([P, T, OG, HD]),
                                      ALU.mult).then_inc(o_normed, 1)
                elif what == "out_proj":
                    a, g = r.batch(half), st[1]
                    dve.wait_ge(wo_done, 2 * a + g + 1)
                    dve.tensor_tensor(flat(x_c[:, 2 * g:2 * g + 2, :]), ps_r[:, g, :],
                                      flat(x_b[:, 2 * g:2 * g + 2, :]), ALU.add).then_inc(x_c_ready, 1)

            def passes(half, r, s):
                if half == "end":
                    return 15
                if s >= 0:
                    return pass_of(r, half)
                return pass_of(r, half) - 1 if not (half == "B" and r.first) else 0

            for st in start_stages:
                emit("start", Start(), st)
            run(dve, emit, link.enter)

        @block.tensor
        def _(pe):
            def three(out_ap, a, b, first, last, check=True):
                n = len(a)
                for i in range(n):
                    (a_hi, a_lo), (b_hi, b_lo) = a[i], b[i]
                    for j, (l, r) in enumerate(((a_hi, b_hi), (a_hi, b_lo), (a_lo, b_hi))):
                        ins = pe.matmul(out_ap, l, r, start=first and i == 0 and j == 0,
                                        stop=last and i == n - 1 and j == 2, skip_group_check=not check)
                return ins

            def emit(half, r, st):
                what = st[0]
                if what == "transpose":
                    n = r.transposed(st[1])
                    if st[1] == "o":
                        pe.wait_ge(o_normed, H // OG * (r.batch(half) + 1))
                        src = x_c
                    else:
                        pe.wait_ge(xn_ready, r.normed(st[1]) + 1)
                        src = xn
                    if half == "start":
                        pe.wait_ge(const_ready, 1)
                    else:
                        pe.wait_ge(xt_lo_done, 2 * n)
                    for kb in range(KB):
                        for i in range(T):
                            ins = pe.transpose(ps_t[:, kb, i * P:(i + 1) * P],
                                               src[:, i, kb * P:(kb + 1) * P], ident[:])
                        ins.then_inc(t_done, 1)
                elif what in ("gate", "up"):
                    s = st[1]
                    u = r.unit(half) + s
                    e, f = s // FB, s % FB
                    xh, xl = (xt_a_hi, xt_a_lo) if half == "A" else (xt_b_hi, xt_b_lo)
                    wh, wl, ps = (wg_hi, wg_lo, ps_g) if what == "gate" else (wu_hi, wu_lo, ps_u)
                    kb = st[2]
                    if kb == 0:
                        if half == "A" and r.first and f == 0:
                            pe.wait_ge(w_ready, (1 if what == "gate" else 2) + 3 * e)
                        if s == 0 and what == "gate":
                            if half == "A":
                                pe.wait_ge(xt_lo_done, 2 if r.first else 2 * (4 * r.k - 2) + 2)
                            else:
                                pe.wait_ge(xt_lo_done, 2 * r.transposed("second") + 2)
                        if not (half == "A" and r.first and s == 0):
                            pe.wait_ge(gated if what == "gate" else h_done, u)
                    cols = slice(f * P, (f + 1) * P)
                    ins = three(ps[:], [(wh[:, e, kb, cols], wl[:, e, kb, cols])],
                                [(xh[:, kb, :], xl[:, kb, :])], kb == 0, kb == KB - 1)
                    if kb == KB - 1:
                        ins.then_inc(g_done if what == "gate" else u_done, 1)
                elif what == "down":
                    u, s = down_unit(half, r, st[1])
                    i = st[2]
                    e, f = s // FB, s % FB
                    if i == 0:
                        if half == "A" and r.first and f == 0:
                            pe.wait_ge(w_ready, 3 * (e + 1))
                        pe.wait_ge(h_lo_done, 2 * u + 1)
                        if f == 0:
                            if not (half == "A" and r.first and e == 0):
                                pe.wait_ge(x_updated, 2 * pass_of(r, half) + e)
                    if i == T // 2:
                        pe.wait_ge(h_lo_done, 2 * u + 2)
                    cols = slice(i * P, (i + 1) * P)
                    ins = three(ps_y[:, i, :], [(h_hi[:, cols], h_lo[:, cols])],
                                [(wd_hi[:, e, f, :], wd_lo[:, e, f, :])], f == 0 and i % 2 == 0,
                                f == FB - 1, check=False)
                    if i == T - 1:
                        ins.then_inc(down_done, 1)
                elif what == "proj":
                    a, c = r.batch(half), st[1]
                    ps = ps_r[:, c % 2, :]
                    if c == 0:
                        pe.wait_ge(xt_lo_done, 2 * r.transposed("attn") + 2)
                        if r.first:
                            pe.wait_ge(w_ready, PIECES)
                    if c >= 2:
                        pe.wait_ge(rest_done, 6 * a + c - 1)
                    elif not r.first:
                        pe.wait_ge(x_c_ready, 2 * a + c - 1)
                    if c < 4:
                        at = (WK if c % 2 else WQ) + (c // 2) * P
                        ins = three(ps, [(wa_hi[:, kb, at:at + P], wa_lo[:, kb, at:at + P]) for kb in range(KB)],
                                    [(xt_a_hi[:, kb, :], xt_a_lo[:, kb, :]) for kb in range(KB)], True, True)
                    else:
                        for t in range(2):
                            i = 2 * (c - 4) + t
                            cols = slice(i * P, (i + 1) * P)
                            ins = three(ps[:, t * D:(t + 1) * D],
                                        [(xt_a_hi[:, kb, cols], xt_a_lo[:, kb, cols]) for kb in range(KB)],
                                        [(wa_hi[:, kb, WV:WV + D], wa_lo[:, kb, WV:WV + D]) for kb in range(KB)],
                                        True, True)
                    ins.then_inc(proj_done, 1)
                elif what == "scores":
                    a, f = r.batch(half), st[1]
                    h = f // 3
                    if f % (3 * HG) == 0:
                        pe.wait_ge(qk_loaded[h // HG], 192 * (a + 1))
                    if f >= 2:
                        pe.wait_ge(max_done, FILLS * a + f - 1)
                    else:
                        pe.wait_ge(rest_done, 6 * a + 5 + f)
                    for i, at in S_FILLS[f % 3]:
                        n = P * (i + 1)
                        ins = pe.matmul(ps_r[:, f % 2, at:at + n], qt[0:ROWS, h, i * P:n],
                                        kt[0:ROWS, h, 0:n], start=True, stop=True)
                    ins.then_inc(s_done, 1)
                elif what == "row_max":
                    a = r.batch(half)
                    pe.wait_ge(max_done, FILLS * (a + 1))
                    last = r.transposed("attn") if r.fixed and r.k == B - 1 else r.transposed("first")
                    pe.wait_ge(xt_lo_done, 2 * last + 2)
                    pe.transpose(ps_m, row_min[:], ident[:]).then_inc(mt_done, 1)
                elif what == "scores_t":
                    a, f = r.batch(half), st[1]
                    h = f // 3
                    if f == 0:
                        pe.wait_ge(max_in, 48 * (a + 1))
                        pe.wait_ge(ones_ready, 1)
                    if f >= 2:
                        pe.wait_ge(exp_done, FILLS * a + f - 1)
                    else:
                        pe.wait_ge(max_done, FILLS * a + FILLS - 1 + f)
                    for j, at in ST_FILLS[f % 3]:
                        n = S - P * j
                        ins = pe.matmul(ps_r[:, f % 2, at:at + n], kt[0:ROWS + 3, h, j * P:(j + 1) * P],
                                        qt[0:ROWS + 3, h, j * P:S], start=True, stop=True)
                    ins.then_inc(st_done, 1)
                elif what == "pv":
                    a, f = r.batch(half), st[1]
                    h = f // 3
                    pe.wait_ge(p_lo_done, FILLS * a + f + 1)
                    if f % 3 == 0 and h >= 2:
                        pe.wait_ge(o_copied, H * a + h - 1)
                    if f == 0:
                        pe.wait_ge(part3_done, 6 * a + 6)
                        pe.wait_ge(max_parts_done, a + 1)
                    for j, at in ST_FILLS[f % 3]:
                        for i in range(j, T):
                            for p in (p_hi, p_lo):
                                ins = pe.matmul(ps_o[h % 2][:, i * VW:(i + 1) * VW],
                                                p[:, f % 4, at + (i - j) * P:at + (i - j + 1) * P],
                                                v_parts[:, j, h, :],
                                                start=(f % 3 == 0 and i == 0 and p is p_hi),
                                                stop=(f % 3 == 2), skip_group_check=True)
                    ins.then_inc(pv_done, 1)
                elif what == "out_proj":
                    a, g = r.batch(half), st[1]
                    if g == 0:
                        pe.wait_ge(xt_lo_done, 2 * r.transposed("o") + 2)
                    pe.wait_ge(exp_done, FILLS * a + FILLS - 1 + g)
                    for t in range(2):
                        i = 2 * g + t
                        cols = slice(i * P, (i + 1) * P)
                        ins = three(ps_r[:, g, t * D:(t + 1) * D],
                                    [(xt_b_hi[:, kb, cols], xt_b_lo[:, kb, cols]) for kb in range(KB)],
                                    [(wa_hi[:, kb, WO:WO + D], wa_lo[:, kb, WO:WO + D]) for kb in range(KB)],
                                    True, True)
                    ins.then_inc(wo_done, 1)

            for st in start_stages:
                emit("start", Start(), st)
            run(pe, emit)


def kernel(L0_attn_x, L0_attn_rms_w, L0_attn_Wq, L0_attn_Wk, L0_attn_Wv, L0_attn_Wo, L0_ffn_gate_w,
           L0_ffn_w_gate, L0_ffn_w_up, L0_ffn_w_down):
    import concourse.bacc as bacc
    import numpy as np
    from concourse.bass_utils import run_bass_kernel_spmd

    def rows(w):
        w = np.asarray(w)
        w = w.reshape(*w.shape[:-2], w.shape[-2] // P, P, w.shape[-1])
        return np.ascontiguousarray(np.moveaxis(w, -2, 0))

    attn = np.concatenate([np.asarray(w) for w in (L0_attn_Wq, L0_attn_Wk, L0_attn_Wv, L0_attn_Wo)], axis=1)
    arrays = {
        "x": np.ascontiguousarray(L0_attn_x),
        "rms_w": np.ascontiguousarray(np.asarray(L0_attn_rms_w).reshape(KB, P).T),
        "gate_w": np.ascontiguousarray(L0_ffn_gate_w),
        "w_gate": rows(np.swapaxes(np.asarray(L0_ffn_w_gate), 1, 2)),
        "w_up": rows(np.swapaxes(np.asarray(L0_ffn_w_up), 1, 2)),
        "w_down": rows(np.swapaxes(np.asarray(L0_ffn_w_down), 1, 2)),
        "w_attn": rows(attn),
    }
    nc = bacc.Bacc("TRN2", target_bir_lowering=False, num_devices=1)
    args = [nc.dram_tensor(n, a.shape, mybir.dt.from_np(a.dtype), kind="ExternalInput").ap()
            for n, a in arrays.items()]
    args.append(nc.dram_tensor("out", (B, S, D), F32, kind="ExternalOutput").ap())
    macaron(nc, *args)
    r = run_bass_kernel_spmd(nc, [arrays], core_ids=[0])
    return r.results[0]["out"]
```

```python
from contextlib import ExitStack

import concourse.bass as bass
from concourse import mybir

F32 = mybir.dt.float32
F32R = mybir.dt.float32r
BF16 = mybir.dt.bfloat16
F16 = mybir.dt.float16
ALU = mybir.AluOpType
ACT = mybir.ActivationFunctionType

P = 128
B, S, D = 8, 512, 256
E, FF = 2, 1024
H = 16
HD = D // H
T = S // P
KB = D // P
FB = FF // P
UNITS = E * FB
EPS = 1e-5
QSCALE = -1.0 / 16.0
HUGE = 3e38
TWO_ONES = 1.0 + 0x3F80 / 2**23
QPART = [0, 1, 2, 0, 1, 0]
KPART = [0, 0, 0, 1, 1, 2]
ROWS = HD * len(QPART)
VW = 3 * HD + 1
FILLS = 3 * H
GROUPS = 2
HG = H // GROUPS
OG = 2
WQ, WK, WV, WO = 0, D, 2 * D, 3 * D
PIECES = 6 * E + 2
STAGES = 8

S_FILLS = [[(3, 0)], [(2, 0), (0, 384)], [(1, 0)]]
ST_FILLS = [[(0, 0)], [(1, 0), (3, 384)], [(2, 0)]]
ST_WIDTH = [512, 512, 256]

DVE_LINKS = {"start": 8, "A0": 0, "A": 36, "B0": 11, "B": 18, "B7": 13}
POOL_LINKS = {"start": 6, "A0": 0, "A": 2, "B0": 5, "B": 5, "B7": 3}


POINTS = 5
PLAN_A = {
    "row_max": 0, "fills": 7, "rate": 1.1, "pauses": [43, 55], "scores_t": 0, "exp": 0, "causal": 0,
    "p_hi": 1, "p_lo": 1, "pv": 4, "out": [66, 66, 69, 69], "second": [70, 71, 72, 75, 76, 77, 77],
}
PLAN_A8 = {
    "fills": 17, "rate": 0.63, "pauses": [35, 48], "scores_t": 0, "exp": 0, "causal": 0, "p_hi": 1,
    "p_lo": 1, "pv": 4, "out": [54, 54, 62, 69], "second": [64, 71, 76, 77, 77, 77, 79], "steps": [0],
}
PLAN_B = {
    "route": [0, 0, 8], "attn": [4, 9, 11, 11, 15, 16, 16], "proj": [19, 19, 20, 22, 25, 27],
    "proj_rest": [20, 20, 24, 25, 26, 34], "qk_in": [23, 39], "residual": [16, 22],
    "first": [28, 30, 31, 38, 39, 45, 48, 54, 60, 64], "scores": 31, "rate": 0.95, "pauses": [42, 52],
}
PLAN_B7 = {
    "route": [0, 0, 0], "attn": [4, 4, 7, 10, 10, 12, 12], "proj": [17, 18, 20, 20, 24, 29],
    "proj_rest": [17, 18, 21, 26, 28, 33], "qk_in": [21, 42], "residual": [11, 12], "scores": 31,
    "rate": 0.93, "pauses": [41, 51], "row_max": 78,
    "steps": [0, 1, 2, 3, 4, 5, 6, 7, 8, 9, 10, 12, 13, 14, 15],
}
PLAN_B0 = {
    "attn": [6, 9, 9, 10, 10, 13, 16], "proj": [17, 19, 20, 24, 25, 27],
    "proj_rest": [19, 19, 25, 26, 29, 29], "qk_in": [21, 49], "residual": [16, 21],
    "first": [22, 26, 28, 30, 36, 40, 42, 47, 47, 53], "scores": 39, "rate": 0.67, "pauses": [13, 51],
}
WEIGHT_STEPS = [0, 1, 1, 1, 2, 2, 3, 9, 10, 10, 13, 13]


def is_round(k, n):
    return isinstance(k, int) and k == n


def half_a(k):
    plan = {}
    at = PLAN_A8 if is_round(k, B) else PLAN_A
    if not is_round(k, 0):
        if not is_round(k, B):
            put(plan, at["row_max"], ("row_max", 0))
        for f in range(FILLS + at["pv"]):
            here = fill_point(at, at["fills"], f)
            for stage in ("pv", "scores_t", "exp", "causal", "p_hi", "p_lo"):
                g = f - at[stage]
                if 0 <= g < FILLS:
                    put(plan, here, (stage, g))
                    if stage == "pv" and g % (3 * OG) == 3 * OG - 1:
                        put(plan, here, ("o_norm", g // (3 * OG)))
        out = [("transpose", "o", 0), ("transpose", "o", 1), ("out_proj", 0), ("out_proj", 1)]
        for where, stage in zip(at["out"], out):
            put(plan, where, stage)
        norm_stages(plan, "second", at["second"])
    else:
        for n, s in enumerate(WEIGHT_STEPS):
            put(plan, s * POINTS + 4, ("weights", 2 + n))
    return steps("A", k, plan)


def half_b(k):
    plan = {}
    at = PLAN_B0 if is_round(k, 0) else PLAN_B7 if is_round(k, B - 1) else PLAN_B
    if not is_round(k, 0):
        for where, stage in zip(at["route"], (("route_a", 0), ("route_a", 1), ("route_b", 0))):
            put(plan, where, (stage[0], "second", stage[1]))
    if not is_round(k, B):
        norm_stages(plan, "attn", at["attn"])
        for c in range(6):
            put(plan, at["proj"][c], ("proj", c))
            put(plan, at["proj_rest"][c], ("proj_rest", c))
        for n in range(2):
            put(plan, at["residual"][n], ("residual", "attn", n))
            put(plan, at["qk_in"][n], ("qk_in", n))
        if not is_round(k, B - 1):
            norm_stages(plan, "first", at["first"])
        for f in range(FILLS):
            put(plan, fill_point(at, at["scores"], f), ("scores", f))
        if is_round(k, 0):
            put(plan, UNITS * POINTS - 1, ("ones", 0))
        if is_round(k, B - 1):
            put(plan, at["row_max"], ("row_max", 0))
    return steps("B", k, plan)


def norm_stages(plan, what, at):
    stages = [("stats", what, 0), ("stats", what, 1), ("rstd", what), ("norm", what, 0), ("norm", what, 1),
              ("transpose", what, 0), ("transpose", what, 1), ("route_a", what, 0), ("route_a", what, 1),
              ("route_b", what)]
    for where, stage in zip(at, stages):
        put(plan, where, stage)


def fill_point(at, start, f):
    here = start + int(f * at["rate"])
    for pause in at["pauses"]:
        here += here >= pause
    return here


def put(plan, where, *stages):
    where = min(where, UNITS * POINTS - 1)
    plan.setdefault((where // POINTS, where % POINTS), []).extend(stages)


def ffn_steps(half, k):
    if half == "B" and is_round(k, 0):
        return {}, 0
    if half == "B" and is_round(k, B - 1):
        return {slot: (None, s) for s, slot in enumerate(PLAN_B7["steps"])}, 0
    if half == "A" and is_round(k, B):
        slots = PLAN_A8["steps"]
        first = UNITS - len(slots)
        return {slot: (("B", B - 1), first + n) for n, slot in enumerate(slots)}, slots[-1] + 1
    ends = not (half == "A" and (is_round(k, 0) or is_round(k, 1)) or half == "B" and is_round(k, B))
    return {s: (None, s) for s in range(UNITS)}, 0 if ends else None


def steps(half, k, plan):
    out = []
    ffn, ending = ffn_steps(half, k)
    for slot in range(UNITS):
        owner, s = ffn.get(slot, (None, None))
        down = (None, -1) if slot == ending else (owner, s - 1) if s else None

        def planned(point):
            out.extend((None, st) for st in plan.get((slot, point), []))

        for kb in range(KB):
            if s is not None:
                out.append((owner, ("gate", s, kb)))
            if kb == 0:
                planned(0)
        for kb in range(KB):
            if s is not None:
                out.append((owner, ("up", s, kb)))
            planned(1 + kb)
        for i in range(T):
            if down:
                out.append((down[0], ("down", down[1], i)))
            if i % 2:
                adds = down and i == T - 1 and down[1] in (-1, FB - 1)
                if adds:
                    out.append((down[0], ("x_update", down[1], 0)))
                    if down[1] == -1:
                        out.append((down[0], ("x_update", down[1], 1)))
                planned(3 + i // 2)
                if adds and down[1] >= 0:
                    out.append((down[0], ("x_update", down[1], 1)))
        if s is not None:
            out.append((owner, ("h_split", s)))
    return out


class Round:

    def __init__(self, k):
        self.k = k
        self.fixed = isinstance(k, int)
        self.first = self.fixed and k == 0
        self.last = self.fixed and k == B

    def unit(self, half):
        if half == "A":
            return 0 if self.first else 32 * self.k - 16
        return 240 if self.last else 16 if self.first else 32 * self.k

    def batch(self, half):
        return self.k - 1 if half == "A" else self.k

    def transposed(self, what):
        if what == "first":
            return 2 if self.first else 4 * self.k + 2
        if what == "attn":
            return 1 if self.first else 4 * self.k + 1
        short = 1 if self.last else 0
        return 4 * self.k - 1 - short if what == "o" else 4 * self.k - short

    def normed(self, what):
        if what == "first":
            return 2 if self.first else 3 * self.k + 2
        if what == "attn":
            return 1 if self.first else 3 * self.k + 1
        return 3 * self.k - (1 if self.last else 0)

    def routed(self, what):
        if what == "first":
            return 1 if self.first else 2 * self.k + 1
        return 2 * self.k - (1 if self.last else 0)


class Start(Round):

    def __init__(self):
        Round.__init__(self, 0)

    def transposed(self, what):
        return 0

    def normed(self, what):
        return 0

    def routed(self, what):
        return 0


class Links:

    def __init__(self, eng, sem, per_part):
        self.eng, self.sem, self.per = eng, sem, per_part
        self.base, self.n, self.part = 0, 0, "start"

    def __call__(self, ins):
        self.n += 1
        ins.then_inc(self.sem, 1)
        self.eng.wait_ge(self.sem, self.base + self.n)

    def enter(self, part, k):
        assert self.n == self.per[self.part], (self.part, self.n)
        p = self.per
        before = p["start"]
        if part != "A0":
            before = before + p["A0"]
            if part != "B0":
                before = before + p["B0"] + (k - 1) * (p["A"] + p["B"])
                if part in ("B", "B7"):
                    before = before + p["A"]
        if part == "A" and isinstance(k, int) and k == B:
            before = before - p["B"] + p["B7"]
        self.base, self.n, self.part = before, 0, part


def macaron(nc, x, rms_w, gate_w, w_gate, w_up, w_down, w_attn, out):
    with ExitStack() as ctx:
        def sb(name, shape, dt):
            return ctx.enter_context(nc.sbuf_tensor(name, shape, dt))

        def sem(name):
            return ctx.enter_context(nc.semaphore(name))

        wg_hi = sb("wg_hi", [P, E, KB, FF], F32R)
        wg_lo = sb("wg_lo", [P, E, KB, FF], F32R)
        wu_hi = sb("wu_hi", [P, E, KB, FF], F32R)
        wu_lo = sb("wu_lo", [P, E, KB, FF], F32R)
        wd_hi = sb("wd_hi", [P, E, FB, D], F32R)
        wd_lo = sb("wd_lo", [P, E, FB, D], F32R)
        wa_hi = sb("wa_hi", [P, KB, 4 * D], F32R)
        wa_lo = sb("wa_lo", [P, KB, 4 * D], F32R)
        x_a = sb("x_a", [P, T, D], F32)
        x_b = sb("x_b", [P, T, D], F32)
        x_c = sb("x_c", [P, T, D], F32)
        xt_a_hi = sb("xt_a_hi", [P, KB, S], F32R)
        xt_a_lo = sb("xt_a_lo", [P, KB, S], F32R)
        xt_b_hi = sb("xt_b_hi", [P, KB, S], F32R)
        xt_b_lo = sb("xt_b_lo", [P, KB, S], F32R)
        hid = sb("hid", [P, 2, S], F32)
        h_hi = sb("h_hi", [P, S], F32R)
        h_lo = sb("h_lo", [P, S], F32R)
        qt = sb("qt", [P, H, S], BF16)
        kt = sb("kt", [P, H, S], BF16)
        v_parts = sb("v_parts", [P, T, H, VW], BF16)
        p_words, split_words, o_words = 3 * S, 4 * S, 2 * T * OG * VW
        area = sb("area", [P, p_words + split_words + o_words], F32)
        p_f32 = area[:, 0:p_words].rearrange("p (r n) -> p r n", r=3)
        p_f16 = area[:, p_words:p_words + split_words].bitcast(F16)
        p_hi = p_f16[:, 0:4 * S].rearrange("p (r n) -> p r n", r=4)
        p_lo = p_f16[:, 4 * S:8 * S].rearrange("p (r n) -> p r n", r=4)
        o_raw = area[:, p_words + split_words:].rearrange("p (g i h c) -> p g i h c", g=2, i=T, h=OG)
        xn = area[:, 0:T * D].rearrange("p (i d) -> p i d", i=T)
        rest = area[:, 0:2 * S].rearrange("p (r n) -> p r n", r=2)
        max_parts = area[:, 0:3 * P // 2].bitcast(BF16).rearrange("p (r n) -> p r n", r=3)
        max_rest = area[:, 2 * P:3 * P]
        qk_parts = area[:, 2 * S:2 * S + 6 * S].bitcast(BF16).rearrange("p (c r n) -> p c r n", c=4, r=3)
        ident = sb("ident", [P, P], F32)
        mask = sb("mask", [P, S], BF16)
        w_diff = sb("w_diff", [P, D], F32)
        rms_col = sb("rms_col", [P, KB], F32)
        minus_half = sb("minus_half", [P, T], F32)
        bn6 = sb("bn6", [P, T, 6], F32)
        mean_var = sb("mean_var", [P, T, 2], F32)
        scales = sb("scales", [P, 2, T], F32)
        shifts = sb("shifts", [P, 2, T], F32)
        minus_mean = sb("minus_mean", [P, T], F32)
        res_scale = sb("res_scale", [P, T], F32)
        tmp_pool = sb("tmp_pool", [P, 2, T], F32)
        dlogit = sb("dlogit", [P, T], F32)
        neg_abs = sb("neg_abs", [P, T], F32)
        e_abs = sb("e_abs", [P, T], F32)
        prob = sb("prob", [P, T], F32)
        coef_a = sb("coef_a", [P, E, T], F32)
        coef_b = sb("coef_b", [P, E, T], F32)
        row_min = sb("row_min", [P, P], F32)
        junk = sb("junk", [P, D], BF16)
        recip = sb("recip", [P, T, OG], F32)

        ps_g = ctx.enter_context(nc.psum_tensor("ps_g", [P, S], F32))
        ps_u = ctx.enter_context(nc.psum_tensor("ps_u", [P, S], F32))
        ps_y = ctx.enter_context(nc.psum_tensor("ps_y", [P, T, D], F32))
        ps_t = ctx.enter_context(nc.psum_tensor("ps_t", [P, KB, S], F32))
        ps_r = ctx.enter_context(nc.psum_tensor("ps_r", [P, 2, S], F32))
        ps_o = [ps_t[:, h, 0:T * VW] for h in range(2)]
        ps_m = ps_t[:, 0, 0:P]
        s_banks = [ps_r[:, 0], ps_r[:, 1], ps_t[:, 1]]

        qk_scratch = nc.dram_tensor("qk_scratch", [4, 3, HG, HD, S], BF16, kind="Internal").ap()
        max_scratch = nc.dram_tensor("max_scratch", [3, T, H, P], BF16, kind="Internal").ap()

        w_in = [sem(f"w_in{n}") for n in range(PIECES)]
        small_in, x_in, x_out = sem("small_in"), sem("x_in"), sem("x_out")
        max_saved, max_in = sem("max_saved"), sem("max_in")
        qk_saved = [sem(f"qk_saved{g}") for g in range(GROUPS)]
        qk_loaded = [sem(f"qk_loaded{g}") for g in range(GROUPS)]
        const_ready, ones_ready, diff_ready = sem("const_ready"), sem("ones_ready"), sem("diff_ready")
        w_hi_done, w_ready = sem("w_hi_done"), sem("w_ready")
        stats_done, rstd_done, res_scale_done = sem("stats_done"), sem("rstd_done"), sem("res_scale_done")
        xn_ready = [sem("xn_ready0"), sem("xn_ready1")]
        t_done, xt_hi_done, xt_lo_done = sem("t_done"), sem("xt_hi_done"), sem("xt_lo_done")
        dlogit_done, e_abs_done = sem("dlogit_done"), sem("e_abs_done")
        g_done, u_done, tanh_done = sem("g_done"), sem("u_done"), sem("tanh_done")
        gated, h_done = sem("gated"), sem("h_done")
        h_hi_done, h_lo_done = sem("h_hi_done"), sem("h_lo_done")
        down_done, x_updated = sem("down_done"), sem("x_updated")
        proj_done, part1_done, rest_done, part2_done, part3_done = (
            sem("proj_done"), sem("part1_done"), sem("rest_done"), sem("part2_done"), sem("part3_done"))
        s_done, max_done, mt_done, max_parts_done = (
            sem("s_done"), sem("max_done"), sem("mt_done"), sem("max_parts_done"))
        st_done, exp_done, causal_done = sem("st_done"), sem("exp_done"), sem("causal_done")
        p_hi_done, p_lo_done, pv_done = sem("p_hi_done"), sem("p_lo_done"), sem("pv_done")
        o_copied, o_normed, wo_done, x_c_ready = sem("o_copied"), sem("o_normed"), sem("wo_done"), sem("x_c_ready")
        dve_link, pool_link = sem("dve_link"), sem("pool_link")
        met_waits = {nc.vector: sem("dve_met"), nc.gpsimd: sem("pool_met"), nc.sync: sem("sp_met")}

        stage = [(qt if n < 4 else kt)[:, 4 * (n % 4):4 * (n % 4) + 4, :].bitcast(F32).rearrange(
            "p (b h) n -> p b (h n)", b=2) for n in range(STAGES)]
        cols = [slice(q * FF // 2, (q + 1) * FF // 2) for q in range(2)]
        blocks = [slice(q * FB // 2, (q + 1) * FB // 2) for q in range(2)]

        def pieces(gate, up, down, attn):
            out = []
            for e in range(E):
                for q in range(2):
                    out += [gate[:, e, :, cols[q]], up[:, e, :, cols[q]],
                            down[:, e, blocks[q], :].rearrange("p (a b) d -> p a (b d)", a=2)]
            return out + [attn[:, kb, :].rearrange("p (a b) -> p a b", a=2) for kb in range(KB)]

        raw = pieces(w_gate, w_up, w_down, w_attn)
        split = list(zip(pieces(wg_hi, wu_hi, wd_hi, wa_hi), pieces(wg_lo, wu_lo, wd_lo, wa_lo)))

        def flat(ap):
            return ap.rearrange("p a b -> p (a b)")

        def xt_of(what):
            return (xt_a_hi, xt_a_lo) if what in ("first", "attn") else (xt_b_hi, xt_b_lo)

        def transposes_bank(half, what, kb):
            return ps_t[:, 0 if half == "B" and what == "first" else kb, :]

        def scores_t_bank(r, f):
            return ps_g[:] if r.last and f % 3 == 2 else ps_r[:, f % (3 if r.last else 2), :]

        def source(what):
            return {"first": x_a, "attn": x_b, "second": x_c}[what]

        def diag(ap):
            return ap.rearrange("p (a b) -> p a b", b=P)[:, 0:4:3, :]

        block = ctx.enter_context(nc.Block())

        def run(eng, emit, enter=None):
            def part(name, half, r):
                if enter and name:
                    enter(name, r.k)
                for owner, st in (half_a if half == "A" else half_b)(r.k):
                    if owner:
                        emit(owner[0], Round(owner[1]), st)
                    else:
                        emit(half, r, st)

            part("A0", "A", Round(0))
            part("B0", "B", Round(0))
            part("A", "A", Round(1))
            part("B", "B", Round(1))
            with eng.Fori(2, B - 1) as k:
                part("A", "A", Round(k))
                part("B", "B", Round(k))
            part("A", "A", Round(B - 1))
            part("B7", "B", Round(B - 1))
            r = Round(B)
            part("A", "A", r)
            part(None, "B", r)
            for i in range(T):
                emit("end", r, ("down", UNITS - 1, i))
            emit("end", r, ("x_update", UNITS - 1, 0))
            emit("end", r, ("x_update", UNITS - 1, 1))

        start_stages = [("stats", "first", 0), ("stats", "first", 1), ("rstd", "first"), ("weights", 0),
                        ("norm", "first", 0), ("norm", "first", 1), ("transpose", "first", 0),
                        ("transpose", "first", 1), ("weights", 1), ("route_a", "first", 0),
                        ("route_a", "first", 1), ("route_b", "first")]
        halves = (range(T // 2), range(T // 2, T))

        def pass_of(r, half):
            if half == "A":
                return 0 if r.first else 2 * r.k - 1
            return 15 if r.last else 2 * r.k

        def met(eng):
            eng.sem_inc(met_waits[eng], 1)

        def down_unit(half, r, s):
            base = r.unit("B") if half == "end" else r.unit(half)
            return base + s, s % UNITS

        @block.sync
        def _(sp):
            def batch_view(ap, n):
                return ap[bass.ds(n, 1)].rearrange("o (i p) d -> p (o i) d", p=P)

            sp.dma_start(x_a[:], batch_view(x, 0)).then_inc(x_in, 16)
            sp.dma_start(x_c[:, 0:E, :], gate_w.partition_broadcast(P)).then_inc(small_in, 16)
            sp.dma_start(rms_col[:], rms_w).then_inc(small_in, 16)
            for n in range(PIECES):
                if n >= STAGES:
                    sp.wait_ge(w_ready, n - STAGES + 1)
                sp.dma_start(stage[n % STAGES], raw[n]).then_inc(w_in[n], 16)

            def emit(half, r, st):
                a = r.batch(half) if half != "end" else None
                if st[0] == "x_update" and st[2] == 1:
                    u, s = down_unit(half, r, st[1])
                    if s != UNITS - 1:
                        return
                    if half == "B":
                        if not (r.last or r.fixed and r.k == B - 1):
                            sp.wait_ge(x_updated, 2 * pass_of(r, "A") + 2)
                            met(sp)
                            sp.dma_start(x_a[:], batch_view(x, r.k + 1)).then_inc(x_in, 16)
                    else:
                        done = 15 if half == "end" else None
                        n = B - 1 if half == "end" else r.k - 2
                        if half == "end":
                            sp.wait_ge(x_updated, 2 * (done + 1))
                        else:
                            sp.wait_ge(x_updated, 2 * (2 * r.k - 2) + 2)
                            met(sp)
                        sp.dma_start(batch_view(out, n), x_c[:]).then_inc(x_out, 16)
                elif st[0] == "proj_rest" and st[1] < 4:
                    c = st[1]
                    sp.wait_ge(part3_done, 6 * a + c + 1)
                    sp.dma_start(qk_scratch[c].rearrange("r h d t -> (h d) r t"),
                                 qk_parts[:, c]).then_inc(qk_saved[c // 2], 16)
                elif st[0] == "qk_in":
                    g = st[1]
                    sp.wait_ge(qk_saved[g], 32 * (a + 1))
                    met(sp)
                    if g == 0:
                        if r.first:
                            sp.wait_ge(w_ready, PIECES)
                        else:
                            sp.wait_ge(st_done, FILLS * a)
                    for n in range(len(QPART)):
                        rows = slice(HD * n, HD * n + HD)
                        heads = slice(HG * g, HG * g + HG)
                        sp.dma_start(qt[rows, heads, :], qk_scratch[2 * g, QPART[n]].rearrange(
                            "h d t -> d h t")).then_inc(qk_loaded[g], 16)
                        sp.dma_start(kt[rows, heads, :], qk_scratch[2 * g + 1, KPART[n]].rearrange(
                            "h d t -> d h t")).then_inc(qk_loaded[g], 16)
                elif st[0] == "row_max":
                    sp.wait_ge(max_parts_done, a + 1)
                    sp.dma_start(max_scratch.rearrange("r i h s -> (i h) r s"),
                                 max_parts[0:T * H]).then_inc(max_saved, 16)
                    sp.wait_ge(max_saved, 16 * (a + 1))
                    for n in range(3):
                        sp.dma_start(qt[ROWS + n:ROWS + n + 1].rearrange("o h (i s) -> o h i s", i=T),
                                     max_scratch[n:n + 1].rearrange("o i h s -> o h i s")
                                     ).then_inc(max_in, 16)

            run(sp, emit)
            sp.wait_ge(x_out, 16 * B)

        @block.gpsimd
        def _(pool):
            link = Links(pool, pool_link, POOL_LINKS)
            link(pool.memset(ident[:], 0.0))
            link(pool.affine_select(out=ident[:], in_=ident[:], compare_op=ALU.not_equal, fill=1.0,
                                    base=0, pattern=[[-1, P]], channel_multiplier=1))
            link(pool.memset(mask[:], 0.0))
            link(pool.affine_select(out=mask[:, S - P:S], in_=mask[:, S - P:S], compare_op=ALU.is_ge,
                                    fill=HUGE, base=0, pattern=[[-1, P]], channel_multiplier=1))
            pool.memset(minus_half[:], -0.5)
            pool.memset(v_parts[:], 1.0)
            pool.memset(row_min[:], 0.0).then_inc(const_ready, 1)
            pool.wait_ge(const_ready, 1)

            def emit(half, r, st):
                if st[0] == "rstd":
                    n = r.normed(st[1])
                    pool.wait_ge(stats_done, n + 1)
                    met(pool)
                    mean, var = mean_var[:, :, 0], mean_var[:, :, 1]
                    both = 1 if st[1] == "attn" else 0
                    if both:
                        pool.tensor_scalar(tmp_pool[:, 1, :], var, 1.0 + EPS, EPS * EPS, ALU.mult, ALU.add)
                    pool.tensor_scalar(tmp_pool[:, 0, :], var, EPS, None, ALU.add)
                    link(pool.tensor_scalar(minus_mean[:], mean, -1.0, None, ALU.mult))
                    link(pool.tensor_tensor(scales[:, both], tmp_pool[:, both], minus_half[:], ALU.pow))
                    pool.tensor_tensor(shifts[:, both], scales[:, both], minus_mean[:],
                                       ALU.mult).then_inc(rstd_done, 1)
                    if both:
                        link(pool.tensor_tensor(scales[:, 0], tmp_pool[:, 0], minus_half[:], ALU.pow))
                        pool.tensor_tensor(shifts[:, 0], scales[:, 0], minus_mean[:], ALU.mult)
                        pool.tensor_scalar(res_scale[:], scales[:, 0], 1.0, None,
                                           ALU.add).then_inc(res_scale_done, 1)
                elif st[0] == "ones":
                    pool.wait_ge(w_ready, PIECES)
                    pool.wait_ge(rstd_done, r.normed("first") + 1)
                    pool.memset(kt[ROWS:ROWS + 3].bitcast(F32), TWO_ONES).then_inc(ones_ready, 1)
                    pool.wait_ge(ones_ready, 1)
                elif st[0] == "h_split":
                    u = r.unit(half) + st[1]
                    pool.wait_ge(h_hi_done, u + 1)
                    for c in (slice(0, S // 2), slice(S // 2, S)):
                        pool.tensor_tensor(h_lo[:, c], hid[:, st[1] % 2, c], h_hi[:, c].bitcast(F32),
                                           ALU.subtract).then_inc(h_lo_done, 1)
                elif st[0] == "causal":
                    f = st[1]
                    pool.wait_ge(exp_done, FILLS * r.batch(half) + f + 1)
                    met(pool)
                    p = p_f32[:, f % 3, :]
                    p = diag(p) if f % 3 == 1 else p[:, 0:P]
                    pool.affine_select(out=p, in_=p, compare_op=ALU.is_ge, fill=0.0, base=0,
                                       pattern=[[0, 2], [1, P]] if f % 3 == 1 else [[1, P]],
                                       channel_multiplier=-1).then_inc(causal_done, 1)

            for st in start_stages:
                emit("start", Start(), st)
            run(pool, emit, link.enter)

        @block.scalar
        def _(act):
            def emit(half, r, st):
                what = st[0]
                if what == "weights":
                    n = st[1]
                    act.wait_ge(w_in[n], 16)
                    act.activation(split[n][0], stage[n % STAGES], ACT.Copy).then_inc(w_hi_done, 1)
                elif what == "norm" and st[2] == 0:
                    act.wait_ge(rstd_done, r.normed(st[1]) + 1)
                    if st[1] == "second":
                        act.wait_ge(p_lo_done, FILLS * (r.batch(half) + 1))
                    elif st[1] == "first" and half == "B":
                        act.wait_ge(part3_done, 6 * r.batch(half) + 6)
                    both = 1 if st[1] == "attn" else 0
                    for i in halves[0]:
                        ins = act.activation(xn[:, i, :], source(st[1])[:, i, :], ACT.Identity,
                                             bias=shifts[:, both, i:i + 1], scale=scales[:, both, i:i + 1])
                    ins.then_inc(xn_ready[0], 1)
                elif what == "transpose":
                    n = r.transposed(st[1])
                    if half == "start" or r.first and st[1] == "attn":
                        act.wait_ge(small_in, 32)
                    kb = st[2]
                    act.wait_ge(t_done, 2 * n + kb + 1)
                    scale = rms_col[:, kb:kb + 1] if st[1] == "attn" else 1.0
                    act.activation(xt_of(st[1])[0][:, kb, :], transposes_bank(half, st[1], kb), ACT.Copy,
                                   scale=scale).then_inc(xt_hi_done, 1)
                elif what == "route_a" and st[2] == 1:
                    act.wait_ge(dlogit_done, r.routed(st[1]) + 1)
                    act.activation(e_abs[:], neg_abs[:], ACT.Exp).then_inc(e_abs_done, 1)
                elif what == "gate" and st[2] == KB - 1:
                    u = r.unit(half) + st[1]
                    act.wait_ge(g_done, u + 1)
                    if not (r.first and half == "A" and st[1] < 2):
                        act.wait_ge(h_lo_done, 2 * u - 2)
                    act.activation(hid[:, st[1] % 2, :], ps_g[:], ACT.Tanh, scale=0.5).then_inc(tanh_done, 1)
                elif what == "h_split":
                    u = r.unit(half) + st[1]
                    act.wait_ge(h_done, u + 1)
                    act.wait_ge(down_done, u)
                    act.activation(h_hi[:], hid[:, st[1] % 2, :], ACT.Copy).then_inc(h_hi_done, 1)
                elif what == "proj":
                    a, c = r.batch(half), st[1]
                    act.wait_ge(proj_done, 6 * a + c + 1)
                    if c < 4:
                        act.activation(qk_parts[:, c, 0, :], ps_r[:, c % 2, :], ACT.Copy,
                                       scale=1.0 if c % 2 else QSCALE).then_inc(part1_done, 1)
                    else:
                        act.activation(v_parts[:, 2 * (c - 4):2 * (c - 4) + 2, :, 0:HD],
                                       ps_r[:, c % 2, :].rearrange("p (i h d) -> p i h d", i=2, h=H),
                                       ACT.Copy).then_inc(part1_done, 1)
                elif what == "proj_rest":
                    a, c = r.batch(half), st[1]
                    act.wait_ge(rest_done, 6 * a + c + 1)
                    if c < 4:
                        act.activation(qk_parts[:, c, 1, :], rest[:, c % 2, :], ACT.Copy).then_inc(part2_done, 1)
                    else:
                        act.activation(v_parts[:, 2 * (c - 4):2 * (c - 4) + 2, :, HD:2 * HD],
                                       rest[:, c % 2, :].rearrange("p (i h d) -> p i h d", i=2, h=H),
                                       ACT.Copy).then_inc(part2_done, 1)
                elif what == "exp":
                    a, f = r.batch(half), st[1]
                    act.wait_ge(st_done, FILLS * a + f + 1)
                    if f >= 3 or not (r.fixed and r.k == 1):
                        act.wait_ge(p_lo_done, FILLS * a + f - 2)
                    n = ST_WIDTH[f % 3]
                    act.activation(p_f32[:, f % 3, 0:n], scores_t_bank(r, f)[:, 0:n], ACT.Exp,
                                   scale=-1.0).then_inc(exp_done, 1)
                elif what == "p_hi" and st[1] % 3:
                    a, f = r.batch(half), st[1]
                    act.wait_ge(causal_done, FILLS * a + f + 1)
                    if f >= 4 or not (r.fixed and r.k == 1):
                        act.wait_ge(pv_done, FILLS * a + f - 3)
                    n = ST_WIDTH[f % 3]
                    act.activation(p_hi[:, f % 4, 0:n], p_f32[:, f % 3, 0:n], ACT.Copy).then_inc(p_hi_done, 1)
                elif what == "pv" and st[1] % 3 == 2:
                    a, h = r.batch(half), st[1] // 3
                    act.wait_ge(pv_done, FILLS * a + 3 * h + 3)
                    if h % OG == 0 and (h >= 2 * OG or not (r.fixed and r.k == 1)):
                        act.wait_ge(o_normed, H // OG * a + h // OG - 1)
                    act.activation(o_raw[:, h // OG % 2, :, h % OG, :], ps_o[h % 2].rearrange("p (i c) -> p i c", i=T),
                                   ACT.Copy).then_inc(o_copied, 1)

            for st in start_stages:
                emit("start", Start(), st)
            run(act, emit)

        @block.vector
        def _(dve):
            link = Links(dve, dve_link, DVE_LINKS)
            dve.wait_ge(small_in, 32)
            dve.tensor_tensor(w_diff[:], x_c[:, 0, :], x_c[:, 1, :], ALU.subtract).then_inc(diff_ready, 1)
            dve.wait_ge(diff_ready, 1)

            def emit(half, r, st):
                what = st[0]
                if what == "weights":
                    n = st[1]
                    dve.wait_ge(w_hi_done, n + 1)
                    dve.tensor_tensor(split[n][1], stage[n % STAGES], split[n][0].bitcast(F32),
                                      ALU.subtract).then_inc(w_ready, 1)
                elif what == "stats":
                    src = source(st[1])
                    if st[1] == "second":
                        dve.wait_ge(x_c_ready, 2 * r.batch(half) + 1 + st[2])
                    elif st[2] == 0 and st[1] == "first":
                        dve.wait_ge(x_in, 16 if half == "start" else 16 * (r.k + 2))
                    elif st[2] == 0:
                        dve.wait_ge(x_updated, 2 * pass_of(r, "A") + 2)
                    for i in halves[st[2]]:
                        ins = dve.bn_stats(bn6[:, i, :], src[:, i, :])
                    if st[2] == 1:
                        link(ins)
                        met(dve)
                        for i in range(T):
                            ins = dve.bn_aggr(mean_var[:, i, :], bn6[:, i, :])
                        ins.then_inc(stats_done, 1)
                elif what == "norm" and st[2] == 1:
                    dve.wait_ge(rstd_done, r.normed(st[1]) + 1)
                    if st[1] == "second":
                        dve.wait_ge(p_lo_done, FILLS * (r.batch(half) + 1))
                    elif st[1] == "first" and half == "B":
                        dve.wait_ge(part3_done, 6 * r.batch(half) + 6)
                    both = 1 if st[1] == "attn" else 0
                    for i in halves[1]:
                        ins = dve.tensor_scalar(xn[:, i, :], source(st[1])[:, i, :], scales[:, both, i:i + 1],
                                                shifts[:, both, i:i + 1], ALU.mult, ALU.add)
                    ins.then_inc(xn_ready[1], 1)
                elif what == "residual":
                    dve.wait_ge(xn_ready[st[2]], r.normed(st[1]) + 1)
                    dve.wait_ge(res_scale_done, r.batch(half) + 1)
                    for i in halves[st[2]]:
                        ins = dve.tensor_scalar(x_b[:, i, :], x_b[:, i, :], res_scale[:, i:i + 1],
                                                shifts[:, 0, i:i + 1], ALU.mult, ALU.add)
                    link(ins)
                elif what == "transpose":
                    n = r.transposed(st[1])
                    hi, lo = xt_of(st[1])
                    kb = st[2]
                    dve.wait_ge(xt_hi_done, 2 * n + kb + 1)
                    bank = transposes_bank(half, st[1], kb)
                    if st[1] == "attn":
                        ins = dve.scalar_tensor_tensor(
                            out=lo[:, kb, :], in0=bank, scalar=rms_col[:, kb:kb + 1],
                            in1=hi[:, kb, :].bitcast(F32), op0=ALU.mult, op1=ALU.subtract)
                    else:
                        ins = dve.tensor_tensor(lo[:, kb, :], bank, hi[:, kb, :].bitcast(F32), ALU.subtract)
                    ins.then_inc(xt_lo_done, 1)
                elif what == "route_a":
                    dve.wait_ge(xn_ready[st[2]], r.normed(st[1]) + 1)
                    for i in halves[st[2]]:
                        link(dve.tensor_tensor_reduce(junk[:], xn[:, i, :], w_diff[:], 1.0, 0.0,
                                                      ALU.mult, ALU.add, dlogit[:, i:i + 1]))
                    if st[2] == 1:
                        dve.scalar_tensor_tensor(out=neg_abs[:], in0=dlogit[:], scalar=-1.0, in1=dlogit[:],
                                                 op0=ALU.mult, op1=ALU.min).then_inc(dlogit_done, 1)
                elif what == "route_b":
                    coef = coef_a if st[1] == "first" else coef_b
                    dve.wait_ge(e_abs_done, r.routed(st[1]) + 1)
                    link(dve.tensor_scalar(prob[:], e_abs[:], 4.0, 4.0, ALU.mult, ALU.add))
                    dve.reciprocal(prob[:], prob[:]).then_inc(dve_link, 1)
                    link.n += 1
                    dve.wait_ge(dve_link, link.base + link.n)
                    dve.scalar_tensor_tensor(out=coef[:, 0, :], in0=dlogit[:], scalar=0.0, in1=prob[:],
                                             op0=ALU.is_ge, op1=ALU.mult)
                    link(dve.scalar_tensor_tensor(out=coef[:, 1, :], in0=dlogit[:], scalar=0.0, in1=prob[:],
                                                  op0=ALU.is_lt, op1=ALU.mult))
                elif what == "up" and st[2] == KB - 1:
                    u = r.unit(half) + st[1]
                    h = hid[:, st[1] % 2, :]
                    dve.wait_ge(tanh_done, u + 1)
                    dve.scalar_tensor_tensor(out=h, in0=h, scalar=1.0, in1=ps_g[:], op0=ALU.add,
                                             op1=ALU.mult).then_inc(gated, 1)
                    dve.wait_ge(gated, u + 1)
                    dve.wait_ge(u_done, u + 1)
                    dve.tensor_tensor(h, h, ps_u[:], ALU.mult).then_inc(h_done, 1)
                elif what == "x_update":
                    u, s = down_unit(half, r, st[1])
                    e = s // FB
                    of_a = (half == "A") == (st[1] >= 0)
                    coef = coef_a if of_a else coef_b
                    src = x_a if of_a else x_c
                    dst = (x_b if of_a else x_c) if e else src
                    if st[2] == 0:
                        dve.wait_ge(down_done, u + 1)
                    if st[2] == 0 and e:
                        dve.wait_ge(x_updated, passes(half, r, st[1]) * 2 + 1)
                    for i in halves[st[2]]:
                        ins = dve.scalar_tensor_tensor(out=dst[:, i, :], in0=ps_y[:, i, :],
                                                       scalar=coef[:, e, i:i + 1], in1=src[:, i, :],
                                                       op0=ALU.mult, op1=ALU.add)
                    if st[2] == 1:
                        ins.then_inc(x_updated, 1)
                elif what == "proj":
                    a, c = r.batch(half), st[1]
                    dve.wait_ge(part1_done, 6 * a + c + 1)
                    if c >= 2:
                        dve.wait_ge(part3_done, 6 * a + c - 1)
                    if c < 4:
                        ins = dve.scalar_tensor_tensor(out=rest[:, c % 2, :], in0=ps_r[:, c % 2, :],
                                                       scalar=1.0 if c % 2 else QSCALE,
                                                       in1=qk_parts[:, c, 0, :], op0=ALU.mult,
                                                       op1=ALU.subtract)
                    else:
                        j = 2 * (c - 4)
                        ins = dve.tensor_tensor(
                            rest[:, c % 2, :].rearrange("p (i h d) -> p i h d", i=2, h=H),
                            ps_r[:, c % 2, :].rearrange("p (i h d) -> p i h d", i=2, h=H),
                            v_parts[:, j:j + 2, :, 0:HD], ALU.subtract)
                    ins.then_inc(rest_done, 1)
                elif what == "proj_rest":
                    a, c = r.batch(half), st[1]
                    dve.wait_ge(part2_done, 6 * a + c + 1)
                    if c < 4:
                        ins = dve.tensor_tensor(qk_parts[:, c, 2, :], rest[:, c % 2, :],
                                                qk_parts[:, c, 1, :], ALU.subtract)
                    else:
                        j = 2 * (c - 4)
                        ins = dve.tensor_tensor(
                            v_parts[:, j:j + 2, :, 2 * HD:3 * HD],
                            rest[:, c % 2, :].rearrange("p (i h d) -> p i h d", i=2, h=H),
                            v_parts[:, j:j + 2, :, HD:2 * HD], ALU.subtract)
                    ins.then_inc(part3_done, 1)
                elif what == "scores":
                    a, f = r.batch(half), st[1]
                    dve.wait_ge(s_done, FILLS * a + f + 1)
                    met(dve)
                    for i, at in S_FILLS[f % 3]:
                        n = P * (i + 1)
                        s = s_banks[f % 3][:, at:at + n]
                        at_min = H * i + f // 3
                        ins = dve.tensor_tensor_reduce(s, s, mask[:, S - n:S], 1.0, HUGE, ALU.add, ALU.min,
                                                       row_min[:, at_min:at_min + 1])
                    ins.then_inc(max_done, 1)
                elif what == "row_max":
                    a = r.batch(half)
                    m = ps_m[0:T * H]
                    parts, left = max_parts[0:T * H], max_rest[0:T * H]
                    dve.wait_ge(mt_done, a + 1)
                    link(dve.tensor_scalar(parts[:, 0, :], m, -1.0, None, ALU.mult))
                    link(dve.scalar_tensor_tensor(out=left, in0=m, scalar=-1.0, in1=parts[:, 0, :],
                                                  op0=ALU.mult, op1=ALU.subtract))
                    link(dve.tensor_copy(parts[:, 1, :], left))
                    dve.tensor_tensor(parts[:, 2, :], left, parts[:, 1, :],
                                      ALU.subtract).then_inc(max_parts_done, 1)
                elif what == "p_lo":
                    a, f = r.batch(half), st[1]
                    n = ST_WIDTH[f % 3]
                    if f % 3:
                        dve.wait_ge(p_hi_done, 2 * H * a + 2 * (f // 3) + f % 3)
                    else:
                        dve.wait_ge(causal_done, FILLS * a + f + 1)
                        if f >= 4 or not (r.fixed and r.k == 1):
                            dve.wait_ge(pv_done, FILLS * a + f - 3)
                        link(dve.tensor_copy(p_hi[:, f % 4, 0:n], p_f32[:, f % 3, 0:n]))
                    dve.tensor_tensor(p_lo[:, f % 4, 0:n], p_f32[:, f % 3, 0:n], p_hi[:, f % 4, 0:n],
                                      ALU.subtract).then_inc(p_lo_done, 1)
                elif what == "o_norm":
                    a, g = r.batch(half), st[1]
                    dve.wait_ge(o_copied, H * a + OG * (g + 1))
                    if g == 0 and not (r.fixed and r.k == 1):
                        dve.wait_ge(x_out, 16 * a)
                    o = x_c[:, :, HD * OG * g:HD * OG * (g + 1)].rearrange("p i (h d) -> p i h d", h=OG)
                    raw_o = o_raw[:, g % 2]
                    dve.tensor_tensor(o, raw_o[:, :, :, 0:HD], raw_o[:, :, :, HD:2 * HD], ALU.add)
                    link(dve.reciprocal(recip[:], raw_o[:, :, :, 3 * HD]))
                    link(dve.tensor_tensor(o, o, raw_o[:, :, :, 2 * HD:3 * HD], ALU.add))
                    dve.tensor_tensor(o, o, recip[:].unsqueeze(3).to_broadcast([P, T, OG, HD]),
                                      ALU.mult).then_inc(o_normed, 1)
                elif what == "out_proj":
                    a, g = r.batch(half), st[1]
                    dve.wait_ge(wo_done, 2 * a + g + 1)
                    dve.tensor_tensor(flat(x_c[:, 2 * g:2 * g + 2, :]), ps_r[:, g, :],
                                      flat(x_b[:, 2 * g:2 * g + 2, :]), ALU.add).then_inc(x_c_ready, 1)

            def passes(half, r, s):
                if half == "end":
                    return 15
                if s >= 0:
                    return pass_of(r, half)
                return pass_of(r, half) - 1 if not (half == "B" and r.first) else 0

            for st in start_stages:
                emit("start", Start(), st)
            run(dve, emit, link.enter)

        @block.tensor
        def _(pe):
            def three(out_ap, a, b, first, last, check=True):
                n = len(a)
                for i in range(n):
                    (a_hi, a_lo), (b_hi, b_lo) = a[i], b[i]
                    for j, (l, r) in enumerate(((a_hi, b_hi), (a_hi, b_lo), (a_lo, b_hi))):
                        ins = pe.matmul(out_ap, l, r, start=first and i == 0 and j == 0,
                                        stop=last and i == n - 1 and j == 2, skip_group_check=not check)
                return ins

            def emit(half, r, st):
                what = st[0]
                if what == "transpose":
                    n, kb = r.transposed(st[1]), st[2]
                    if kb == 0:
                        if st[1] == "o":
                            pe.wait_ge(o_normed, H // OG * (r.batch(half) + 1))
                        else:
                            pe.wait_ge(xn_ready[0], r.normed(st[1]) + 1)
                        if half == "start":
                            pe.wait_ge(const_ready, 1)
                        else:
                            pe.wait_ge(xt_lo_done, 2 * n)
                    elif half == "B" and st[1] == "first":
                        pe.wait_ge(xt_lo_done, 2 * n + 1)
                    src = x_c if st[1] == "o" else xn
                    bank = transposes_bank(half, st[1], kb)
                    for i in range(T):
                        if kb == 0 and i == T // 2 and st[1] != "o":
                            pe.wait_ge(xn_ready[1], r.normed(st[1]) + 1)
                        ins = pe.transpose(bank[:, i * P:(i + 1) * P], src[:, i, kb * P:(kb + 1) * P], ident[:])
                    ins.then_inc(t_done, 1)
                elif what in ("gate", "up"):
                    s = st[1]
                    u = r.unit(half) + s
                    e, f = s // FB, s % FB
                    xh, xl = (xt_a_hi, xt_a_lo) if half == "A" else (xt_b_hi, xt_b_lo)
                    wh, wl, ps = (wg_hi, wg_lo, ps_g) if what == "gate" else (wu_hi, wu_lo, ps_u)
                    kb = st[2]
                    if kb == 0:
                        if half == "A" and r.first and f % (FB // 2) == 0:
                            pe.wait_ge(w_ready, (1 if what == "gate" else 2) + 6 * e + 3 * (2 * f // FB))
                        if s == 0 and what == "gate":
                            if half == "A":
                                pe.wait_ge(xt_lo_done, 2 if r.first else 2 * (4 * r.k - 2) + 2)
                            else:
                                pe.wait_ge(xt_lo_done, 2 * r.transposed("second") + 2)
                        if half == "B" and r.last and s == 0 and what == "gate":
                            pe.wait_ge(exp_done, FILLS * B)
                        if not (half == "A" and r.first and s == 0):
                            pe.wait_ge(gated if what == "gate" else h_done, u)
                    cols = slice(f * P, (f + 1) * P)
                    ins = three(ps[:], [(wh[:, e, kb, cols], wl[:, e, kb, cols])],
                                [(xh[:, kb, :], xl[:, kb, :])], kb == 0, kb == KB - 1)
                    if kb == KB - 1:
                        ins.then_inc(g_done if what == "gate" else u_done, 1)
                elif what == "down":
                    u, s = down_unit(half, r, st[1])
                    i = st[2]
                    e, f = s // FB, s % FB
                    if i == 0:
                        if half == "A" and r.first and f % (FB // 2) == 0:
                            pe.wait_ge(w_ready, 3 + 6 * e + 3 * (2 * f // FB))
                        pe.wait_ge(h_lo_done, 2 * u + 1)
                        if f == 0:
                            if not (half == "A" and r.first and e == 0):
                                pe.wait_ge(x_updated, 2 * pass_of(r, half) + e)
                    if i == T // 2:
                        pe.wait_ge(h_lo_done, 2 * u + 2)
                    cols = slice(i * P, (i + 1) * P)
                    ins = three(ps_y[:, i, :], [(h_hi[:, cols], h_lo[:, cols])],
                                [(wd_hi[:, e, f, :], wd_lo[:, e, f, :])], f == 0 and i % 2 == 0,
                                f == FB - 1, check=False)
                    if i == T - 1:
                        ins.then_inc(down_done, 1)
                elif what == "proj":
                    a, c = r.batch(half), st[1]
                    ps = ps_r[:, c % 2, :]
                    if c == 0:
                        pe.wait_ge(xt_lo_done, 2 * r.transposed("attn") + 2)
                        if r.first:
                            pe.wait_ge(w_ready, PIECES)
                    if c >= 2:
                        pe.wait_ge(rest_done, 6 * a + c - 1)
                    elif not r.first:
                        pe.wait_ge(x_c_ready, 2 * a + c - 1)
                    if c < 4:
                        at = (WK if c % 2 else WQ) + (c // 2) * P
                        ins = three(ps, [(wa_hi[:, kb, at:at + P], wa_lo[:, kb, at:at + P]) for kb in range(KB)],
                                    [(xt_a_hi[:, kb, :], xt_a_lo[:, kb, :]) for kb in range(KB)], True, True)
                    else:
                        for t in range(2):
                            i = 2 * (c - 4) + t
                            cols = slice(i * P, (i + 1) * P)
                            ins = three(ps[:, t * D:(t + 1) * D],
                                        [(xt_a_hi[:, kb, cols], xt_a_lo[:, kb, cols]) for kb in range(KB)],
                                        [(wa_hi[:, kb, WV:WV + D], wa_lo[:, kb, WV:WV + D]) for kb in range(KB)],
                                        True, True)
                    ins.then_inc(proj_done, 1)
                elif what == "scores":
                    a, f = r.batch(half), st[1]
                    h = f // 3
                    if f % (3 * HG) == 0:
                        pe.wait_ge(qk_loaded[h // HG], 192 * (a + 1))
                    if f >= 3:
                        pe.wait_ge(max_done, FILLS * a + f - 2)
                    else:
                        pe.wait_ge(rest_done, 6 * a + 5 + min(f, 1))
                    for i, at in S_FILLS[f % 3]:
                        n = P * (i + 1)
                        ins = pe.matmul(s_banks[f % 3][:, at:at + n], qt[0:ROWS, h, i * P:n],
                                        kt[0:ROWS, h, 0:n], start=True, stop=True)
                    ins.then_inc(s_done, 1)
                elif what == "row_max":
                    a = r.batch(half)
                    pe.wait_ge(max_done, FILLS * (a + 1))
                    before = r.transposed("o") if half == "A" else r.transposed("attn") + 1
                    pe.wait_ge(xt_lo_done, 2 * before)
                    pe.transpose(ps_m, row_min[:], ident[:]).then_inc(mt_done, 1)
                elif what == "scores_t":
                    a, f = r.batch(half), st[1]
                    h = f // 3
                    if f == 0:
                        pe.wait_ge(max_in, 48 * (a + 1))
                        pe.wait_ge(ones_ready, 1)
                    banks = 3 if r.last else 2
                    if f == 0:
                        pe.wait_ge(max_done, FILLS * (a + 1))
                    elif f == 2 and r.last:
                        pe.wait_ge(gated, r.unit(half))
                    elif f >= banks:
                        pe.wait_ge(exp_done, FILLS * a + f - banks + 1)
                    for j, at in ST_FILLS[f % 3]:
                        n = S - P * j
                        ins = pe.matmul(scores_t_bank(r, f)[:, at:at + n], kt[0:ROWS + 3, h, j * P:(j + 1) * P],
                                        qt[0:ROWS + 3, h, j * P:S], start=True, stop=True)
                    ins.then_inc(st_done, 1)
                elif what == "pv":
                    a, f = r.batch(half), st[1]
                    h = f // 3
                    pe.wait_ge(p_lo_done, FILLS * a + f + 1)
                    if f % 3 == 0 and h >= 2:
                        pe.wait_ge(o_copied, H * a + h - 1)
                    if f == 0:
                        pe.wait_ge(part3_done, 6 * a + 6)
                        pe.wait_ge(max_parts_done, a + 1)
                    for j, at in ST_FILLS[f % 3]:
                        for i in range(j, T):
                            for p in (p_hi, p_lo):
                                ins = pe.matmul(ps_o[h % 2][:, i * VW:(i + 1) * VW],
                                                p[:, f % 4, at + (i - j) * P:at + (i - j + 1) * P],
                                                v_parts[:, j, h, :],
                                                start=(f % 3 == 0 and i == 0 and p is p_hi),
                                                stop=(f % 3 == 2), skip_group_check=True)
                    ins.then_inc(pv_done, 1)
                elif what == "out_proj":
                    a, g = r.batch(half), st[1]
                    if g == 0:
                        pe.wait_ge(xt_lo_done, 2 * r.transposed("o") + 2)
                    pe.wait_ge(exp_done, FILLS * a + FILLS - 1 + g)
                    for t in range(2):
                        i = 2 * g + t
                        cols = slice(i * P, (i + 1) * P)
                        ins = three(ps_r[:, g, t * D:(t + 1) * D],
                                    [(xt_b_hi[:, kb, cols], xt_b_lo[:, kb, cols]) for kb in range(KB)],
                                    [(wa_hi[:, kb, WO:WO + D], wa_lo[:, kb, WO:WO + D]) for kb in range(KB)],
                                    True, True)
                    ins.then_inc(wo_done, 1)

            for st in start_stages:
                emit("start", Start(), st)
            run(pe, emit)


def kernel(L0_attn_x, L0_attn_rms_w, L0_attn_Wq, L0_attn_Wk, L0_attn_Wv, L0_attn_Wo, L0_ffn_gate_w,
           L0_ffn_w_gate, L0_ffn_w_up, L0_ffn_w_down):
    import concourse.bacc as bacc
    import numpy as np
    from concourse.bass_utils import run_bass_kernel_spmd

    def rows(w):
        w = np.asarray(w)
        w = w.reshape(*w.shape[:-2], w.shape[-2] // P, P, w.shape[-1])
        return np.ascontiguousarray(np.moveaxis(w, -2, 0))

    attn = np.concatenate([np.asarray(w) for w in (L0_attn_Wq, L0_attn_Wk, L0_attn_Wv, L0_attn_Wo)], axis=1)
    arrays = {
        "x": np.ascontiguousarray(L0_attn_x),
        "rms_w": np.ascontiguousarray(np.asarray(L0_attn_rms_w).reshape(KB, P).T),
        "gate_w": np.ascontiguousarray(L0_ffn_gate_w),
        "w_gate": rows(np.swapaxes(np.asarray(L0_ffn_w_gate), 1, 2)),
        "w_up": rows(np.swapaxes(np.asarray(L0_ffn_w_up), 1, 2)),
        "w_down": rows(np.swapaxes(np.asarray(L0_ffn_w_down), 1, 2)),
        "w_attn": rows(attn),
    }
    nc = bacc.Bacc("TRN2", target_bir_lowering=False, num_devices=1)
    args = [nc.dram_tensor(n, a.shape, mybir.dt.from_np(a.dtype), kind="ExternalInput").ap()
            for n, a in arrays.items()]
    args.append(nc.dram_tensor("out", (B, S, D), F32, kind="ExternalOutput").ap())
    macaron(nc, *args)
    r = run_bass_kernel_spmd(nc, [arrays], core_ids=[0])
    return r.results[0]["out"]
```
